# Optimizing a Trainium2 kernel written in Bass

```python
import numpy as np
import jax
import jax.numpy as jnp

def _softmax(x, axis=-1):
    return jax.nn.softmax(x, axis=axis)

def _gelu(x):
    return jax.nn.gelu(x, approximate=True)

def _silu(x):
    return jax.nn.silu(x)

def _sigmoid(x):
    return jax.nn.sigmoid(x)

def _layernorm(x, axis=-1, eps=1e-05):
    m = jnp.mean(x, axis=axis, keepdims=True)
    v = jnp.var(x, axis=axis, keepdims=True)
    return (x - m) / jnp.sqrt(v + eps)

def _scatter_add(tgt, idx, src, axis=0):
    return tgt.at[idx].add(src)

def _segment_sum(src, seg, n):
    return jax.ops.segment_sum(src, seg, n)
kernel_name = 'mk_conv_seq_d1_conv_nchw384_r4_c4e9e3'

def setup_inputs(seed: int=0):
    np.random.seed(seed)
    _w = jnp.asarray

    def _rec_inputs():
        import jax
        import jax.numpy as jnp
        _gk = jax.random.key(seed)
        x = -0.0001476 + 0.9999 * jax.random.normal(jax.random.fold_in(_gk, 1), (32, 96, 56, 56), jnp.float32)
        return x
    x = _rec_inputs()

    def _L0_conv_setup():
        import jax, jax.numpy as jnp
        from jax import lax
        import numpy as np
        DIM = 96
        HEADS = 12
        WS = 7
        HEAD_DIM = DIM // HEADS
        SCALE = HEAD_DIM ** (-0.5)
        HIDDEN = 4 * DIM
        EPS = 1e-05
        _c = np.arange(WS)
        _cf = np.stack(np.meshgrid(_c, _c, indexing='ij'), axis=-1).reshape(-1, 2)
        _rel = _cf[:, None, :] - _cf[None, :, :] + (WS - 1)
        REL_IDX = jnp.asarray(_rel[..., 0] * (2 * WS - 1) + _rel[..., 1])

        def _layernorm(x, g, b):
            mu = x.mean(-1, keepdims=True)
            var = jnp.mean((x - mu) ** 2, axis=-1, keepdims=True)
            return (x - mu) * lax.rsqrt(var + EPS) * g + b

        def _attention(xw, ln_g, ln_b, qkv_w, qkv_b, proj_w, proj_b, bias_table):
            Bw, N, C = xw.shape
            xn = _layernorm(xw, ln_g, ln_b)
            qkv = (xn @ qkv_w.T + qkv_b).reshape(Bw, N, 3, HEADS, HEAD_DIM)
            qkv = qkv.transpose(2, 0, 3, 1, 4)
            q, k, v = (qkv[0], qkv[1], qkv[2])
            attn = jnp.einsum('bhnd,bhmd->bhnm', q * SCALE, k)
            bias = bias_table[REL_IDX]
            attn = attn + bias.transpose(2, 0, 1)[None]
            attn = jax.nn.softmax(attn, axis=-1)
            out = jnp.einsum('bhnm,bhmd->bhnd', attn, v)
            out = out.transpose(0, 2, 1, 3).reshape(Bw, N, C)
            return out @ proj_w.T + proj_b
        key = jax.random.key(seed)
        ks = jax.random.split(key, 8)
        s = 0.02
        return {'x': jax.random.normal(ks[0], (32, DIM, 56, 56), dtype=jnp.float32), 'ln_g': jnp.ones((DIM,), jnp.float32), 'ln_b': jnp.zeros((DIM,), jnp.float32), 'qkv_w': jax.random.normal(ks[1], (3 * DIM, DIM), jnp.float32) * s, 'qkv_b': jnp.zeros((3 * DIM,), jnp.float32), 'proj_w': jax.random.normal(ks[2], (DIM, DIM), jnp.float32) * s, 'proj_b': jnp.zeros((DIM,), jnp.float32), 'bias_table': jax.random.normal(ks[3], ((2 * WS - 1) ** 2, HEADS), jnp.float32) * s, 'conv_w': jax.random.normal(ks[4], (DIM, 1, 3, 3), jnp.float32) * 0.1, 'bn_g': jnp.ones((DIM,), jnp.float32), 'bn_b': jnp.zeros((DIM,), jnp.float32), 'bn_mean': jnp.zeros((DIM,), jnp.float32), 'bn_var': jnp.ones((DIM,), jnp.float32), 'w1': jax.random.normal(ks[5], (HIDDEN, DIM), jnp.float32) * s, 'b1': jnp.zeros((HIDDEN,), jnp.float32), 'w2': jax.random.normal(ks[6], (DIM, HIDDEN), jnp.float32) * s, 'b2': jnp.zeros((DIM,), jnp.float32), 'H': 56, 'W': 56}
    _L0_conv_all = _L0_conv_setup()
    _L0_conv_in = {k: v for k, v in _L0_conv_all.items() if k in ('ln_g', 'ln_b', 'qkv_w', 'qkv_b', 'proj_w', 'proj_b', 'bias_table', 'conv_w', 'bn_g', 'bn_b', 'bn_mean', 'bn_var', 'w1', 'b1', 'w2', 'b2')}
    del _L0_conv_all
    return {'x': x, 'L0_conv_ln_g': _L0_conv_in['ln_g'], 'L0_conv_ln_b': _L0_conv_in['ln_b'], 'L0_conv_qkv_w': _L0_conv_in['qkv_w'], 'L0_conv_qkv_b': _L0_conv_in['qkv_b'], 'L0_conv_proj_w': _L0_conv_in['proj_w'], 'L0_conv_proj_b': _L0_conv_in['proj_b'], 'L0_conv_bias_table': _L0_conv_in['bias_table'], 'L0_conv_conv_w': _L0_conv_in['conv_w'], 'L0_conv_bn_g': _L0_conv_in['bn_g'], 'L0_conv_bn_b': _L0_conv_in['bn_b'], 'L0_conv_bn_mean': _L0_conv_in['bn_mean'], 'L0_conv_bn_var': _L0_conv_in['bn_var'], 'L0_conv_w1': _L0_conv_in['w1'], 'L0_conv_b1': _L0_conv_in['b1'], 'L0_conv_w2': _L0_conv_in['w2'], 'L0_conv_b2': _L0_conv_in['b2']}

def reference(x, L0_conv_ln_g, L0_conv_ln_b, L0_conv_qkv_w, L0_conv_qkv_b, L0_conv_proj_w, L0_conv_proj_b, L0_conv_bias_table, L0_conv_conv_w, L0_conv_bn_g, L0_conv_bn_b, L0_conv_bn_mean, L0_conv_bn_var, L0_conv_w1, L0_conv_b1, L0_conv_w2, L0_conv_b2):
    import jax
    import jax.numpy as jnp

    def _L0_conv_ref(x, ln_g, ln_b, qkv_w, qkv_b, proj_w, proj_b, bias_table, conv_w, bn_g, bn_b, bn_mean, bn_var, w1, b1, w2, b2, H, W):
        import jax, jax.numpy as jnp
        from jax import lax
        import numpy as np
        DIM = 96
        HEADS = 12
        WS = 7
        HEAD_DIM = DIM // HEADS
        SCALE = HEAD_DIM ** (-0.5)
        HIDDEN = 4 * DIM
        EPS = 1e-05
        _c = np.arange(WS)
        _cf = np.stack(np.meshgrid(_c, _c, indexing='ij'), axis=-1).reshape(-1, 2)
        _rel = _cf[:, None, :] - _cf[None, :, :] + (WS - 1)
        REL_IDX = jnp.asarray(_rel[..., 0] * (2 * WS - 1) + _rel[..., 1])

        def _layernorm(x, g, b):
            mu = x.mean(-1, keepdims=True)
            var = jnp.mean((x - mu) ** 2, axis=-1, keepdims=True)
            return (x - mu) * lax.rsqrt(var + EPS) * g + b

        def _attention(xw, ln_g, ln_b, qkv_w, qkv_b, proj_w, proj_b, bias_table):
            Bw, N, C = xw.shape
            xn = _layernorm(xw, ln_g, ln_b)
            qkv = (xn @ qkv_w.T + qkv_b).reshape(Bw, N, 3, HEADS, HEAD_DIM)
            qkv = qkv.transpose(2, 0, 3, 1, 4)
            q, k, v = (qkv[0], qkv[1], qkv[2])
            attn = jnp.einsum('bhnd,bhmd->bhnm', q * SCALE, k)
            bias = bias_table[REL_IDX]
            attn = attn + bias.transpose(2, 0, 1)[None]
            attn = jax.nn.softmax(attn, axis=-1)
            out = jnp.einsum('bhnm,bhmd->bhnd', attn, v)
            out = out.transpose(0, 2, 1, 3).reshape(Bw, N, C)
            return out @ proj_w.T + proj_b
        B, C, H_in, W_in = x.shape
        seq = x.reshape(B, C, H * W).transpose(0, 2, 1)
        shortcut = seq
        if H <= WS and W <= WS:
            out = _attention(seq, ln_g, ln_b, qkv_w, qkv_b, proj_w, proj_b, bias_table)
        else:
            pad_b = -H % WS
            pad_r = -W % WS
            x_pad = x if pad_b == 0 and pad_r == 0 else jnp.pad(x, ((0, 0), (0, 0), (0, pad_b), (0, pad_r)))
            H_pad, W_pad = (H + pad_b, W + pad_r)
            nH, nW = (H_pad // WS, W_pad // WS)
            xw = x_pad.reshape(B, C, nH, WS, nW, WS)
            xw = xw.transpose(0, 2, 4, 3, 5, 1).reshape(B * nH * nW, WS * WS, C)
            ow = _attention(xw, ln_g, ln_b, qkv_w, qkv_b, proj_w, proj_b, bias_table)
            ow = ow.reshape(B, nH, nW, WS, WS, C).transpose(0, 5, 1, 3, 2, 4)
            out_full = ow.reshape(B, C, H_pad, W_pad)
            if pad_b > 0 or pad_r > 0:
                out_full = out_full[:, :, :H, :W]
            out = out_full.reshape(B, C, H * W).transpose(0, 2, 1)
        seq = shortcut + out
        x_local = seq.transpose(0, 2, 1).reshape(B, C, H, W)
        conv = lax.conv_general_dilated(x_local, conv_w, (1, 1), ((1, 1), (1, 1)), dimension_numbers=('NCHW', 'OIHW', 'NCHW'), feature_group_count=DIM)
        scale = (bn_g * lax.rsqrt(bn_var + EPS))[None, :, None, None]
        bn = (conv - bn_mean[None, :, None, None]) * scale + bn_b[None, :, None, None]
        seq2 = bn.reshape(B, C, H * W).transpose(0, 2, 1)
        h = jax.nn.gelu(seq2 @ w1.T + b1, approximate=False)
        seq = seq2 + (h @ w2.T + b2)
        return seq.transpose(0, 2, 1).reshape(B, C, H, W)

    def _gn(v, G=32, eps=1e-05):
        B_, C_, H_, W_ = v.shape
        g = v.reshape(B_, G, C_ // G, H_, W_)
        m = jnp.mean(g, axis=(2, 3, 4), keepdims=True)
        s = jnp.var(g, axis=(2, 3, 4), keepdims=True)
        return ((g - m) / jnp.sqrt(s + eps)).reshape(v.shape)

    def _ln_c(v, eps=1e-06):
        m = jnp.mean(v, axis=1, keepdims=True)
        s = jnp.var(v, axis=1, keepdims=True)
        return (v - m) / jnp.sqrt(s + eps)

    def _ln_t(v, eps=1e-05):
        m = jnp.mean(v, axis=-1, keepdims=True)
        s = jnp.var(v, axis=-1, keepdims=True)
        return (v - m) / jnp.sqrt(s + eps)

    def _to_tokens(v):
        B_, C_, H_, W_ = v.shape
        return v.reshape(B_, C_, H_ * W_).transpose(0, 2, 1)

    def _from_tokens(t, like):
        B_, C_, H_, W_ = like.shape
        return t.transpose(0, 2, 1).reshape(B_, C_, H_, W_)
    x = _L0_conv_ref(x, L0_conv_ln_g, L0_conv_ln_b, L0_conv_qkv_w, L0_conv_qkv_b, L0_conv_proj_w, L0_conv_proj_b, L0_conv_bias_table, L0_conv_conv_w, L0_conv_bn_g, L0_conv_bn_b, L0_conv_bn_mean, L0_conv_bn_var, L0_conv_w1, L0_conv_b1, L0_conv_w2, L0_conv_b2, 56, 56)
    return x

_drawn_inputs = setup_inputs


def setup_inputs(seed=0):
    import zlib

    import numpy as np

    out = dict(_drawn_inputs(seed))
    spreads = {'L0_conv_ln_g': (1.0, 0.6),
     'L0_conv_ln_b': (0.0, 0.8),
     'L0_conv_qkv_b': (0.0, 0.542),
     'L0_conv_proj_b': (0.0, 0.1),
     'L0_conv_bn_g': (1.0, 0.2),
     'L0_conv_bn_b': (0.0, 0.1),
     'L0_conv_bn_mean': (0.0, 0.1),
     'L0_conv_bn_var': (1.0, 0.2),
     'L0_conv_b1': (0.0, 0.1),
     'L0_conv_b2': (0.0, 0.1)}
    factors = {'L0_conv_qkv_w': 8.0, 'L0_conv_proj_w': 2.861, 'L0_conv_bias_table': 8.0}
    for name, (base, spread) in spreads.items():
        noise = np.random.default_rng([zlib.crc32(name.encode()), seed]).standard_normal(out[name].shape)
        drawn = base * np.exp(spread * noise) if base else spread * noise
        out[name] = jnp.asarray(drawn.astype(out[name].dtype))
    for name, factor in factors.items():
        out[name] = (out[name] * factor).astype(out[name].dtype)
    return out
```

```python
from contextlib import ExitStack

import numpy as np

import concourse.bass as bass
from concourse import mybir

F32, F16 = mybir.dt.float32, mybir.dt.float16
ALU, ACT, AX = mybir.AluOpType, mybir.ActivationFunctionType, mybir.AxisListType

BATCH, C, SIDE, WS, HEADS = 32, 96, 56, 7, 12
HD = C // HEADS
SCALE = HD ** -0.5
HID = 4 * C
NB = HID // 128
EPS = 1e-5
TOK = WS * WS
NW = SIDE // WS
NP = NW // 2
CT = NW * TOK
CPI = SIDE // WS
CHUNKS = BATCH * CPI
WP = 64
NJ = HEADS // 2
ROWS = 64 + TOK
PIECE = 16
VW = HD + 1
PAD = SIDE + 2
CROW = WS * PAD
STEPS = CHUNKS + 6
UN = 4


def block_program(nc, x, w_qkv, b_qkv_row, b_v, w_proj, w_proj2, b_proj_row, ln_g, ln_b, bias_q, bias_k,
                  conv_w, bn_g, bn_b, bn_mean, bn_var, w1, b1, w2, b2, eye, out):
    ctx = ExitStack()
    with ctx:
        def sb(name, shape, dt=F32):
            return ctx.enter_context(nc.sbuf_tensor(name, shape, dt))

        def sem(name):
            return ctx.enter_context(nc.semaphore(name))

        def sems(name, n):
            return [sem(f"{name}{i}") for i in range(n)]

        wq_h, wq_l = sb("wq_h", [97, 3 * C], F16), sb("wq_l", [97, 3 * C], F16)
        wp_h, wp_l = sb("wp_h", [97, 4, C], F16), sb("wp_l", [97, 4, C], F16)
        wpn_f = sb("wpn_f", [C, C])
        cols = sb("cols", [C, 24])
        b1_c = sb("b1_c", [128, NB])
        w1_h, w1_l = sb("w1_h", [C, HID], F16), sb("w1_l", [C, HID], F16)
        w2_f = sb("w2_f", [128, NB * C])
        w2_h, w2_l = sb("w2_h", [128, NB, C], F16), sb("w2_l", [128, NB, C], F16)
        eye_f, eye_h = sb("eye_f", [128, 128]), sb("eye_h", [128, 128], F16)
        center, avg = sb("center", [C, C]), sb("avg", [C, C])
        lo_l = sb("lo_l", [TOK, HEADS * TOK], F16)
        hot_f, hot_h = sb("hot_f", [ROWS, WP]), sb("hot_h", [ROWS, WP], F16)
        hot2 = sb("hot2", [TOK, 2, WP], F16)
        g_c, b_c, bv_c, bng_c, bnb_c, bnm_c, bnv_c, b2_c = (cols[:, i:i + 1] for i in range(8))
        sc_c, cb_c, bvs_c, eps_c = (cols[:, i:i + 1] for i in range(8, 12))
        cw_c = cols[:, 12:21]
        x_sb = sb("x_sb", [C, CPI * CT])
        sq, rstd = sb("sq", [C, CT]), sb("rstd", [C, CT])
        xn = sb("xn", [C, NW, TOK])
        xh, xl = sb("xh", [97, 2, NW, WP], F16), sb("xl", [97, 2, NW, WP], F16)
        qh, ql, kh, kl = (sb(n, [C, 2, NW * WP], F16) for n in ("qh", "ql", "kh", "kl"))
        k_st = sb("k_st", [ROWS, 4, NJ, NW * WP], F16)
        q_bd = sb("q_bd", [ROWS, 4, HEADS, NW * WP], F16)
        q_st = sb("q_st", [ROWS, 2, NJ, NW * WP], F16)
        k_bd = sb("k_bd", [ROWS, 2, HEADS, NW * WP], F16)
        vh, vl = sb("vh", [128, 4, HEADS, NW, VW], F16), sb("vl", [128, 4, HEADS, NW, VW], F16)
        mx, mxt = sb("mx", [128, 2, HEADS, NP], F16), sb("mxt", [HEADS * NP, 2, 128], F16)
        p32 = sb("p32", [128, 2, HEADS, TOK])
        ph, pl = sb("ph", [128, 2, HEADS, WP], F16), sb("pl", [128, 2, HEADS, WP], F16)
        rec = sb("rec", [128, 2, 2, HEADS])
        on = sb("on", [128, NP, C])
        oh, ol = sb("oh", [97, NP, 2, WP], F16), sb("ol", [97, NP, 2, WP], F16)
        ximg = sb("ximg", [C, PAD * PAD + 4])
        s2 = sb("s2", [97, 2, CT])
        s2h, s2l = sb("s2h", [C, CT], F16), sb("s2l", [C, CT], F16)
        g32 = sb("g32", [128, NB, CT])
        gh, gl = sb("gh", [128, NB, CT], F16), sb("gl", [128, NB, CT], F16)
        y = sb("y", [C, 2, CT])
        bias_f = p32[0:ROWS, :, :, :].rearrange("p a h t -> p a (h t)")
        bias_h = gl[0:ROWS, :, :].rearrange("p k t -> p (k t)").rearrange("p (a c) -> p a c", a=2)
        lo_f = g32[0:TOK, :, :].rearrange("p k t -> p (k t)")[:, 0:HEADS * TOK]
        wg_f = g32[0:97, :, :].rearrange("p k t -> p (k t)")[:, HEADS * TOK:HEADS * TOK + 3 * C]
        lo_h = gh[0:TOK, :, :].rearrange("p k t -> p (k t)")[:, 0:HEADS * TOK]
        wp_f, rows_f = s2[:, 0, 0:4 * C], s2[:, 1, 0:4 * C]
        w1_f, wq_f = y[:, 0, 0:HID], y[:, 1, 0:3 * C]

        st_ps = ctx.enter_context(nc.psum_tensor("st_ps", [128, 2, 512], F32))
        sm_ps = ctx.enter_context(nc.psum_tensor("sm_ps", [128, 2, 512], F32))
        o_ps = ctx.enter_context(nc.psum_tensor("o_ps", [128, 512], F32))
        a_ps = ctx.enter_context(nc.psum_tensor("a_ps", [128, 512], F32))
        b_ps = ctx.enter_context(nc.psum_tensor("b_ps", [128, 512], F32))
        d_ps = ctx.enter_context(nc.psum_tensor("d_ps", [128, 512], F32))
        mxt_ps = sm_ps[0:HEADS * NP, 0, 0:64].bitcast(F16)
        HALF = NJ // 2 * 2 * TOK

        loaded = sem("loaded")
        dve_setup, act_setup, pe_setup, pool_setup = sem("dve_setup"), sem("act_setup"), sem("pe_setup"), sem("pool_setup")
        ready = sem("ready")
        x_in = sems("x_in", 4)
        max_in = sems("max_in", 2)
        exp_in = sems("exp_in", 4)
        row_in = sems("row_in", 2)
        stored = sems("stored", 2)
        xc_done, sq_done, var_done, lnv_done, rstd_done, xn_done, xh_done, xl_done = (sem(n) for n in (
            "xc_done", "sq_done", "var_done", "lnv_done", "rstd_done", "xn_done", "xh_done", "xl_done"))
        q_done, k_done, qh_done, kh_done, ql_done, kl_done = (sem(n) for n in (
            "q_done", "k_done", "qh_done", "kh_done", "ql_done", "kl_done"))
        v_done, vh_done, vl_done = sem("v_done"), sem("vh_done"), sem("vl_done")
        sm_done, max_done, mxt_done, mxt_out = sem("sm_done"), sem("max_done"), sem("mxt_done"), sem("mxt_out")
        st_done, p32_done, ph_done, pl_done = sem("st_done"), sem("p32_done"), sem("ph_done"), sem("pl_done")
        pv_done, rec_done, norm_done = sem("pv_done"), sem("rec_done"), sem("norm_done")
        ot_done, oh_done, ol_done, proj_done, sum_done = (sem(n) for n in (
            "ot_done", "oh_done", "ol_done", "proj_done", "sum_done"))
        tap0_done, tap_done, s2h_done, s2l_done = sem("tap0_done"), sem("tap_done"), sem("s2h_done"), sem("s2l_done")
        hid_done, g32_done, gh_done, gl_done = sem("hid_done"), sem("g32_done"), sem("gh_done"), sem("gl_done")
        mlp_done, y_done = sem("mlp_done"), sem("y_done")

        def real(st, lag):
            u, e = st
            return not isinstance(u, int) or 0 <= UN * u + e - lag < CHUNKS

        def wait(eng, s, st, lag, per=1, k=None):
            u, e = st
            v = u * (UN * per) + ((e - lag) * per + (per if k is None else k))
            if not isinstance(v, int) or v > 0:
                eng.wait_ge(s, v)

        def wait_ring(eng, ring, st, lag, per=16):
            u, e = st
            n = len(ring)
            v = u * (UN // n * per) + ((e - lag) // n + 1) * per
            if not isinstance(v, int) or v > 0:
                eng.wait_ge(ring[(e - lag) % n], v)

        def place(st, lag):
            u, e = st
            g = u + (e - lag) // UN
            return g // 2, g % 2 * UN + (e - lag) % UN

        def dram_place(st, lag):
            img, r = place(st, lag)
            return (img, r * CT) if isinstance(img, int) else (nc.sync.snap(img), nc.sync.snap(r * CT))

        def run(eng, step):
            for s in range(2 * UN):
                step((s // UN, s % UN))
            with eng.Fori(2, CHUNKS // UN - 1) as u:
                for e in range(UN):
                    step((u, e))
            for s in range(CHUNKS - UN, STEPS):
                step((s // UN, s % UN))

        def exp_pair(p):
            return (3, 3) if p == 0 else (2, p - 1)

        def pv_pair(p):
            return (3, p + 2) if p < 2 else (2, p - 2)

        x_v = x.rearrange("b c h w -> c b (h w)")
        out_v = out.rearrange("b c h w -> c b (h w)")

        def image_order(ap, width):
            return ap.rearrange("c (r w k) -> c w r k", w=NW, k=WS) if width == SIDE else \
                ap.rearrange("c (r q) -> c r q", q=width)[:, :, 0:SIDE].rearrange("c r (w k) -> c w r k", k=WS)

        def image_rows(st, lag, dy, dx):
            _, r = place(st, lag)
            return ximg[:, bass.ds(r * CROW + (dy * PAD + dx), CROW)].rearrange("c (r q) -> c r q", q=PAD)[:, :, 0:SIDE]

        block = ctx.enter_context(nc.Block())

        @block.sync
        def _(sp):
            loads = [
                (wq_f[0:C, :], w_qkv), (rows_f[96:97, 0:3 * C], b_qkv_row), (rows_f[96:97, 3 * C:], b_proj_row),
                (bv_c, b_v), (wpn_f[:, :], w_proj), (g_c, ln_g), (b_c, ln_b), (bng_c, bn_g), (bnb_c, bn_b),
                (bnm_c, bn_mean), (bnv_c, bn_var), (b2_c, b2), (cw_c, conv_w), (b1_c[:, :], b1), (w1_f[:, :], w1),
                (w2_f[:, :].rearrange("p (k c) -> p k c", k=NB), w2), (eye_f[:, :], eye),
                (bias_f[64:ROWS, 0, :], bias_q), (bias_f[64:ROWS, 1, :], bias_k), (lo_f[:, :], bias_q),
                (hot_f[64:ROWS, :], eye[0:TOK, 0:WP]),
            ]
            sp.wait_ge(pool_setup, 1)
            for w in range(2):
                for h2 in range(2):
                    loads.append((wp_f[48 * w:48 * w + 48, (2 * w + h2) * C:(2 * w + h2 + 1) * C], w_proj2[h2]))
            for dst, src in loads:
                sp.dma_start(dst, src).then_inc(loaded, 16)
            sp.wait_ge(loaded, 16 * len(loads))

            def load(c):
                sp.dma_start(x_sb[:, c * CT:(c + 1) * CT], x_v[:, 0, c * CT:(c + 1) * CT]).then_inc(x_in[c % 4], 16)

            for c in range(3):
                load(c)
            sp.wait_ge(ready, 4)

            def held(v):
                return v if isinstance(v, int) else nc.sync.snap(v)

            def count(st, lag, per=1):
                u, e = st
                return held(u * (UN * per) + (e - lag + 1) * per)

            def wait_for(s, v):
                if not isinstance(v, int) or v > 0:
                    sp.wait_ge(s, v)

            def step(st):
                e = st[1]
                c0, c1, c5, c6 = (count(st, lag) for lag in (0, 1, 5, 6))
                if real(st, -3):
                    img, at = dram_place(st, -3)
                    wait_for(sum_done, c5)
                    sp.dma_start(x_sb[:, bass.ds(at, CT)], x_v[:, bass.ds(img, 1), bass.ds(at, CT)]
                                 .rearrange("c b k -> c (b k)")).then_inc(x_in[(e + 3) % 4], 16)
                if real(st, 6):
                    img, at = dram_place(st, 6)
                    wait_for(y_done, c6)
                    sp.dma_start(out_v[:, bass.ds(img, 1), bass.ds(at, CT)].rearrange("c b k -> c (b k)"),
                                 y[:, (e - 6) % 2, :]).then_inc(stored[(e - 6) % 2], 16)
                if real(st, 0):
                    r2, r4 = e % 2, e % 4
                    wait_for(qh_done, c0)
                    sp.dma_start(q_st[16:32, r2, :, :], qh[:, r2, :]).then_inc(max_in[r2], 16)
                    wait_for(kh_done, c0)
                    for h2 in range(2):
                        sp.dma_start(k_bd[16 + 8 * h2:24 + 8 * h2, r2, h2::2, :], kh[48 * h2:48 * h2 + 48, r2, :])\
                          .then_inc(max_in[r2], 16)
                    wait_for(ql_done, c0)
                    wait_for(kl_done, c0)
                    for n, (kk, qq) in enumerate(((kh, qh), (kl, qh), (kh, ql))):
                        r0 = PIECE * (n + 1)
                        sp.dma_start(k_st[r0:r0 + PIECE, r4, :, :], kk[:, r2, :]).then_inc(exp_in[r4], 16)
                        for h2 in range(2):
                            sp.dma_start(q_bd[r0 + 8 * h2:r0 + 8 * h2 + 8, r4, h2::2, :],
                                         qq[48 * h2:48 * h2 + 48, r2, :]).then_inc(exp_in[r4], 16)
                if real(st, 1):
                    wait_for(mxt_out, c1)
                    sp.dma_start(q_bd[0:1, (e - 1) % 4, :, :].rearrange("p h (n c) -> p (h n) c", c=2 * WP),
                                 mxt[:, (e - 1) % 2, :]).then_inc(row_in[(e - 1) % 2], 16)

            run(sp, step)
            for r in stored:
                sp.wait_ge(r, 16 * (CHUNKS // 2))

        @block.tensor
        def _(pe):
            mm = nc.tensor.matmul

            def three(o, sh, sl, mh, ml, start=True, stop=True):
                mm(o, sh, mh, start=start, stop=False)
                mm(o, sh, ml, start=False, stop=False)
                return mm(o, sl, mh, start=False, stop=stop)

            pe.wait_ge(loaded, 16 * 25)
            mm(a_ps[96:97, 0:3 * C], b_c, wq_f[0:C, :], start=True, stop=True)
            mm(b_ps[0:C, 0:1], wq_f[0:C, 2 * C:], b_c, start=True, stop=True).then_inc(pe_setup, 1)
            pe.wait_ge(dve_setup, 2)
            mm(d_ps[96:97, 0:C], bvs_c, wpn_f[:, :], start=True, stop=True).then_inc(pe_setup, 1)
            pe.wait_ge(ready, 4)

            def exp_scores(st, lag, q):
                e = st[1]
                if q == 0:
                    wait_ring(pe, exp_in, st, lag, 9 * 16)
                    wait_ring(pe, row_in, st, lag)
                wait(pe, ph_done, st, lag, NP, q)
                r = (e - lag) % 4
                for b in range(2):
                    mm(st_ps[:, b, 0:HALF], hot2[:, :, :].rearrange("p a b -> p (a b)"), lo_l[:, b * HALF:(b + 1) * HALF],
                       start=True, stop=False, skip_group_check=True)
                for j in range(NJ):
                    for w in range(2):
                        n = (2 * q + w) * WP
                        c0 = j % (NJ // 2) * 2 * TOK
                        last = mm(st_ps[64 * w:64 * w + 64, j // (NJ // 2), c0:c0 + 2 * TOK], k_st[:, r, j, n:n + WP],
                                  q_bd[:, r, 2 * j:2 * j + 2, n:n + TOK], start=False, stop=True, skip_group_check=True)
                last.then_inc(st_done, 1)

            def max_scores(st, p):
                e = st[1]
                if p == 0:
                    wait_ring(pe, max_in, st, 1, 3 * 16)
                    wait(pe, mxt_out, st, 2)
                wait(pe, max_done, st, 1, NP, p)
                r = (e - 1) % 2
                for j in range(NJ):
                    for w in range(2):
                        n = (2 * p + w) * WP
                        c0 = j % (NJ // 2) * 2 * TOK
                        last = mm(sm_ps[64 * w:64 * w + 64, j // (NJ // 2), c0:c0 + 2 * TOK], q_st[:, r, j, n:n + WP],
                                  k_bd[:, r, 2 * j:2 * j + 2, n:n + TOK], start=True, stop=True)
                last.then_inc(sm_done, 1)

            def values_times_p(st, lag, q):
                e = st[1]
                if q == 0:
                    wait(pe, vl_done, st, lag, 2)
                wait(pe, pl_done, st, lag, NP, q + 1)
                if q % 2 == 0:
                    wait(pe, norm_done, st, lag, 4, q)
                r, r2 = (e - lag) % 4, q % 2
                for j in range(NJ):
                    o = o_ps[:, r2 * 256:r2 * 256 + 2 * HEADS * VW].rearrange("p (w h) -> p w h", w=2)[:, :, j * 2 * VW:(j + 1) * 2 * VW]

                    def moving(v):
                        return v[:, r, 2 * j:2 * j + 2, 2 * q:2 * q + 2, :].rearrange("p h w d -> p w h d")

                    s_h = ph[:, r2, 2 * j:2 * j + 2, :].rearrange("p h n -> p (h n)")
                    s_l = pl[:, r2, 2 * j:2 * j + 2, :].rearrange("p h n -> p (h n)")
                    last = three(o, s_h, s_l, moving(vh), moving(vl))
                last.then_inc(pv_done, 1)

            def step(st):
                e = st[1]
                for p in range(NP):
                    lag, q = exp_pair(p)
                    if real(st, lag):
                        exp_scores(st, lag, q)
                    if real(st, 1):
                        max_scores(st, p)
                    if p == 0 and real(st, 0):
                        wait_ring(pe, x_in, st, 0)
                        wait(pe, sum_done, st, 4)
                        _, r = place(st, 0)
                        mm(a_ps[0:C, 0:CT], center[:, :], x_sb[:, bass.ds(r * CT, CT)], start=True, stop=True).then_inc(xc_done, 1)
                    if p == 0 and real(st, 1):
                        wait(pe, gh_done, st, 6, NB)
                        wait(pe, ql_done, st, 1)
                        r = (e - 1) % 2
                        for n in range(NP):
                            s_h = xh[0:C, r, 2 * n:2 * n + 2, :].rearrange("c w n -> c (w n)")
                            s_l = xl[0:C, r, 2 * n:2 * n + 2, :].rearrange("c w n -> c (w n)")
                            last = three(b_ps[:, n * C:(n + 1) * C], s_h, s_l, wq_h[0:C, 2 * C:], wq_l[0:C, 2 * C:])
                        last.then_inc(v_done, 1)
                    if p == 1 and real(st, 6):
                        wait(pe, gl_done, st, 6, NB)
                        for k in range(NB):
                            last = three(d_ps[0:C, 0:CT], w2_h[:, k, :], w2_l[:, k, :], gh[:, k, :], gl[:, k, :],
                                         start=k == 0, stop=k == NB - 1)
                        last.then_inc(mlp_done, 1)
                    if p == 1 and real(st, 0):
                        wait(pe, sq_done, st, 0)
                        wait(pe, vl_done, st, 1, 2)
                        mm(b_ps[0:C, 0:CT], avg[:, :], sq[:, :], start=True, stop=True).then_inc(var_done, 1)
                    if p == 2 and real(st, 3):
                        wait(pe, norm_done, st, 3, 4)
                        wait(pe, xn_done, st, 0) if real(st, 0) else None
                        for n in range(NP):
                            last = nc.tensor.transpose(a_ps[0:C, n * 128:(n + 1) * 128], on[:, n, :], eye_f[:, :])
                        last.then_inc(ot_done, 1)
                    if p == 2 and real(st, 0):
                        wait(pe, xl_done, st, 0)
                        r = e % 2
                        m_h, m_l = xh[:, r, :, 0:TOK], xl[:, r, :, 0:TOK]
                        three(b_ps[0:C, 0:CT], wq_h[:, 0:C], wq_l[:, 0:C], m_h, m_l).then_inc(q_done, 1)
                        wait(pe, y_done, st, 6)
                        three(d_ps[0:C, 0:CT], wq_h[:, C:2 * C], wq_l[:, C:2 * C], m_h, m_l).then_inc(k_done, 1)
                    if p == 3 and real(st, 3):
                        wait(pe, ol_done, st, 3)
                        for w in range(2):
                            o = a_ps[0:C, 0:CT].rearrange("c (n w t) -> c w n t", w=2, t=TOK)[:, w]
                            for h2 in range(2):
                                last = three(o, wp_h[:, 2 * w + h2, :], wp_l[:, 2 * w + h2, :],
                                             oh[:, :, h2, 0:TOK], ol[:, :, h2, 0:TOK], start=h2 == 0, stop=h2 == 1)
                        last.then_inc(proj_done, 1)
                    if p == 3 and real(st, 5):
                        wait(pe, s2l_done, st, 5)
                        for k in range(NB):
                            if k == 0:
                                wait(pe, ql_done, st, 0) if real(st, 0) else None
                            if k == 1:
                                wait(pe, kl_done, st, 0) if real(st, 0) else None
                            if k == 2:
                                wait(pe, gh_done, st, 5, NB, 1)
                                if real(st, 1):
                                    wait(pe, max_done, st, 1, NP)
                            t = b_ps if k % 2 == 0 else d_ps
                            three(t[:, 0:CT], w1_h[:, k * 128:(k + 1) * 128], w1_l[:, k * 128:(k + 1) * 128],
                                  s2h[:, :], s2l[:, :]).then_inc(hid_done, 1)
                    if p == 3 and real(st, 1):
                        if not real(st, 5):
                            wait(pe, max_done, st, 1, NP)
                        nc.tensor.transpose(mxt_ps, mx[:, (e - 1) % 2, :, :].rearrange("p h n -> p (h n)"), eye_h[:, :])\
                          .then_inc(mxt_done, 1)
                    lag, q = pv_pair(p)
                    if real(st, lag):
                        values_times_p(st, lag, q)

            run(pe, step)

        @block.scalar
        def _(act):
            af = nc.scalar.activation
            act.wait_ge(loaded, 16 * 25)
            act.wait_ge(dve_setup, 1)
            af(sc_c, bnv_c, ACT.Ln, bias=eps_c).then_inc(act_setup, 1)
            act.wait_ge(act_setup, 1)
            af(sc_c, sc_c, ACT.Exp, scale=-0.5).then_inc(act_setup, 1)
            act.wait_ge(ready, 4)

            def exps(st, lag, q):
                wait(act, st_done, st, lag, NP, q + 1)
                wait(act, pl_done, st, lag, NP, q - 1)
                src = st_ps[:, :, 0:HALF].rearrange("p b (h n) -> p b h n", n=TOK)
                af(p32[:, q % 2, :, :].rearrange("p (b h) n -> p b h n", b=2), src, ACT.Exp).then_inc(p32_done, 1)
                wait(act, pv_done, st, lag, NP, q - 1)
                af(ph[:, q % 2, :, 0:TOK].rearrange("p (b h) n -> p b h n", b=2), src, ACT.Exp).then_inc(ph_done, 1)

            def step(st):
                e = st[1]
                for p in range(NP):
                    if p == 2 and real(st, 0):
                        wait(act, xn_done, st, 0)
                        wait(act, v_done, st, 2)
                        af(xh[0:C, e % 2, :, 0:TOK], xn[:, :, :], ACT.Identity).then_inc(xh_done, 1)
                    lag, q = exp_pair(p)
                    if real(st, lag):
                        exps(st, lag, q)
                    if p == 0 and real(st, 0):
                        wait(act, xc_done, st, 0)
                        wait(act, var_done, st, 1)
                        af(sq[:, :], a_ps[0:C, 0:CT], ACT.Square).then_inc(sq_done, 1)
                    if p == 0 and real(st, 1):
                        wait(act, v_done, st, 1)
                        wait(act, pv_done, st, 5, NP)
                        for w in range(2):
                            af(vh[64 * w:64 * w + TOK, (e - 1) % 4, :, w::2, 0:HD],
                               b_ps[64 * w:64 * w + TOK, 0:NP * C].rearrange("p (n h d) -> p h n d", n=NP, d=HD),
                               ACT.Identity).then_inc(vh_done, 1)
                    if p == 0 and real(st, 5):
                        if real(st, 4):
                            wait(act, sum_done, st, 4)
                        wait(act, y_done, st, 7)
                        af(s2[0:C, (e - 5) % 2, :].rearrange("c (r q) -> c r q", q=SIDE), image_rows(st, 5, 0, 0),
                           ACT.Identity, bias=cb_c, scale=cw_c[:, 0:1]).then_inc(tap0_done, 1)
                    if p == 1 and real(st, 0):
                        wait(act, var_done, st, 0)
                        wait(act, xn_done, st, 1)
                        af(rstd[:, :], b_ps[0:C, 0:CT], ACT.Ln, bias=eps_c).then_inc(lnv_done, 1)
                        wait(act, lnv_done, st, 0)
                        af(rstd[:, :], rstd[:, :], ACT.Exp, scale=-0.5).then_inc(rstd_done, 1)
                    if p == 2 and real(st, 3):
                        wait(act, ot_done, st, 3)
                        wait(act, proj_done, st, 4)
                        af(oh[0:C, :, :, :].rearrange("c n a t -> c (n a t)"), a_ps[0:C, :], ACT.Identity).then_inc(oh_done, 1)
                    if p == 3 and real(st, 0):
                        wait_ring(act, exp_in, st, 2, 9 * 16)
                        wait_ring(act, max_in, st, 2, 3 * 16)
                        for ps, dst, done, out_ in ((b_ps, qh, q_done, qh_done), (d_ps, kh, k_done, kh_done)):
                            wait(act, done, st, 0)
                            af(dst[:, e % 2, :].rearrange("c (w t) -> c w t", t=WP)[:, :, 0:TOK],
                               ps[0:C, 0:CT].rearrange("c (w t) -> c w t", t=TOK), ACT.Identity).then_inc(out_, 1)
                    if p == 3 and real(st, 5):
                        wait(act, tap_done, st, 5, 8)
                        wait(act, hid_done, st, 6, NB)
                        af(s2h[:, :], s2[0:C, (e - 5) % 2, :], ACT.Identity).then_inc(s2h_done, 1)
                        wait(act, mlp_done, st, 6)
                        for k in range(NB):
                            t = b_ps if k % 2 == 0 else d_ps
                            wait(act, hid_done, st, 5, NB, k + 1)
                            wait(act, gl_done, st, 6, NB)
                            af(g32[:, k, :], t[:, 0:CT], ACT.Gelu, bias=b1_c[:, k:k + 1]).then_inc(g32_done, 1)
                            af(gh[:, k, :], t[:, 0:CT], ACT.Gelu, bias=b1_c[:, k:k + 1]).then_inc(gh_done, 1)

            run(act, step)

        @block.gpsimd
        def _(pool):
            tt = nc.gpsimd.tensor_tensor
            nc.gpsimd.memset(wp_f[:, :], 0.0).then_inc(pool_setup, 1)
            for t in (q_bd, xh, xl, oh, ol, qh, ql, kh, kl, ph, pl, on):
                nc.gpsimd.memset(t[:], 0.0)
            nc.gpsimd.memset(ximg[:, :], 0.0).then_inc(pool_setup, 1)
            pool.wait_ge(pool_setup, 2)
            nc.gpsimd.memset(xh[96:97, :, :, :], 1.0)
            nc.gpsimd.memset(oh[96:97, :, :, :], 1.0).then_inc(pool_setup, 1)
            pool.wait_ge(pool_setup, 3)
            pool.sem_inc(ready, 1)
            pool.wait_ge(ready, 4)

            def step(st):
                e = st[1]
                for p in range(NP):
                    if p == 2 and real(st, 0):
                        wait(pool, xh_done, st, 0)
                        tt(xl[0:C, e % 2, :, 0:TOK], xn[:, :, :], xh[0:C, e % 2, :, 0:TOK], ALU.subtract).then_inc(xl_done, 1)
                    lag, q = exp_pair(p)
                    if real(st, lag):
                        wait(pool, ph_done, st, lag, NP, q + 1)
                        wait(pool, pv_done, st, lag, NP, q - 1)
                        tt(pl[:, q % 2, :, 0:TOK], p32[:, q % 2, :, :], ph[:, q % 2, :, 0:TOK], ALU.subtract).then_inc(pl_done, 1)
                    if p == 3 and real(st, 5):
                        wait(pool, s2h_done, st, 5)
                        tt(s2l[:, :], s2[0:C, (e - 5) % 2, :], s2h[:, :], ALU.subtract).then_inc(s2l_done, 1)
                        for k in range(NB):
                            wait(pool, gh_done, st, 5, NB, k + 1)
                            tt(gl[:, k, :], g32[:, k, :], gh[:, k, :], ALU.subtract).then_inc(gl_done, 1)

            run(pool, step)

        @block.vector
        def _(dve):
            v = nc.vector
            at = [0]

            def link(ins):
                at[0] += 1
                ins.then_inc(dve_setup, 1)
                dve.wait_ge(dve_setup, at[0])

            link(v.memset(eps_c, EPS))
            dve.wait_ge(loaded, 16 * 25)
            dve.wait_ge(pe_setup, 1)
            link(v.tensor_tensor(bvs_c, b_ps[0:C, 0:1], bv_c, ALU.add))
            link(v.tensor_scalar(wg_f[0:C, :], wq_f[0:C, :], g_c, None, ALU.mult))
            link(v.tensor_tensor(wg_f[96:97, :], a_ps[96:97, 0:3 * C], rows_f[96:97, 0:3 * C], ALU.add))
            link(v.tensor_scalar(wg_f[:, 0:C], wg_f[:, 0:C], SCALE, None, ALU.mult))
            dve.wait_ge(pe_setup, 2)
            for w in range(2):
                link(v.tensor_tensor(wp_f[96:97, 2 * w * C:(2 * w + 1) * C], d_ps[96:97, 0:C], rows_f[96:97, 3 * C:], ALU.add))
            link(v.memset(hot2[:, :, :], 0.0))
            for w in range(2):
                link(v.tensor_copy(hot2[:, w, 0:TOK], eye_f[0:TOK, 0:TOK]))
            for f, h, l in ((wg_f[:, :], wq_h[:, :], wq_l[:, :]), (wp_f[:, :], wp_h[:, :, :].rearrange("p a c -> p (a c)"),
                            wp_l[:, :, :].rearrange("p a c -> p (a c)")), (w1_f[:, :], w1_h[:, :], w1_l[:, :]),
                            (w2_f[:, :], w2_h[:, :, :].rearrange("p a c -> p (a c)"), w2_l[:, :, :].rearrange("p a c -> p (a c)")),
                            (lo_f[:, :], lo_h[:, :], lo_l[:, :])):
                link(v.tensor_copy(h, f))
                link(v.tensor_tensor(l, f, h, ALU.subtract))
            link(v.tensor_copy(eye_h[:, :], eye_f[:, :]))
            link(v.tensor_scalar(center[:, :], eye_f[0:C, 0:C], -1.0 / C, None, ALU.add))
            link(v.memset(avg[:, :], 1.0 / C))
            dve.wait_ge(act_setup, 2)
            link(v.tensor_tensor(sc_c, sc_c, bng_c, ALU.mult))
            link(v.tensor_scalar(cw_c, cw_c, sc_c, None, ALU.mult))
            link(v.tensor_tensor(cb_c, bnm_c, sc_c, ALU.mult))
            link(v.tensor_tensor(cb_c, bnb_c, cb_c, ALU.subtract))
            for t in (q_st, k_st, k_bd, vh, vl):
                link(v.memset(t[:], 0.0))
            dve.wait_ge(pool_setup, 3)
            link(v.tensor_copy(hot_h[64:ROWS, :], hot_f[64:ROWS, :]))
            link(v.tensor_copy(bias_h[64:ROWS, :, :], bias_f[64:ROWS, :, :]))
            for r in range(4):
                for t, n, which in ((k_st, 4, None), (q_st, 2, None), (q_bd, 4, 0), (k_bd, 2, 1)):
                    if r >= n:
                        continue
                    if which is None:
                        link(v.tensor_copy(t[64:ROWS, r, :, :].rearrange("p j (w t) -> p (j w) t", t=WP),
                                           hot_h[64:ROWS, :].unsqueeze(1).broadcast_to([TOK, NJ * NW, WP])))
                    else:
                        link(v.tensor_copy(t[64:ROWS, r, :, :].rearrange("p h (w t) -> p h w t", t=WP)[:, :, :, 0:TOK],
                                           bias_h[64:ROWS, which, :].rearrange("p (h t) -> p h t", t=TOK)
                                           .unsqueeze(2).broadcast_to([TOK, HEADS, NW, TOK])))
                link(v.memset(k_st[0:1, r, :, :].rearrange("p j (w t) -> p (j w) t", t=WP)[:, :, 0:TOK], -1.0))
                for w in range(2):
                    link(v.memset(vh[64 * w:64 * w + TOK, r, :, w::2, HD:VW], 1.0))
            dve.sem_inc(ready, 3)

            def maxima(st, p):
                wait(dve, sm_done, st, 1, NP, p + 1)
                wait(dve, mxt_done, st, 3)
                v.tensor_reduce(mx[:, (st[1] - 1) % 2, :, p].rearrange("p (b h) -> p b h", b=2),
                                sm_ps[:, :, 0:HALF].rearrange("p b (h n) -> p b h n", n=TOK), AX.X, ALU.max)\
                 .then_inc(max_done, 1)

            def normalise(st, half):
                wait(dve, pv_done, st, 3, NP, 2 * half + 2)
                wait(dve, ot_done, st, 4)
                o = o_ps[:, :].rearrange("p (n c) -> p n c", n=2)[:, :, 0:2 * HEADS * VW].rearrange("p n (g a d) -> p n g a d", a=2, d=VW)
                for h2 in range(2):
                    rows = slice(64 * h2, 64 * h2 + TOK)
                    v.reciprocal(rec[rows, half, :, :], o[rows, :, :, h2, HD]).then_inc(rec_done, 1)
                for h2 in range(2):
                    rows = slice(64 * h2, 64 * h2 + TOK)
                    wait(dve, rec_done, st, 3, 4, 2 * half + h2 + 1)
                    v.tensor_tensor(on[rows, 2 * half:2 * half + 2, :].rearrange("p n (g d) -> p n g d", d=HD),
                                    o[rows, :, :, h2, 0:HD], rec[rows, half, :, :].unsqueeze(3).broadcast_to([TOK, 2, HEADS, HD]),
                                    ALU.mult).then_inc(norm_done, 1)

            def taps(st, ks):
                acc = s2[0:C, (st[1] - 5) % 2, :].rearrange("c (r q) -> c r q", q=SIDE)
                for k in ks:
                    if k == 1:
                        wait(dve, tap0_done, st, 5)
                    else:
                        wait(dve, tap_done, st, 5, 8, k - 1)
                    v.scalar_tensor_tensor(acc, image_rows(st, 5, k // 3, k % 3), cw_c[:, k:k + 1], acc, ALU.mult, ALU.add)\
                     .then_inc(tap_done, 1)

            def step(st):
                e = st[1]
                if real(st, 3):
                    normalise(st, 0)
                if real(st, 1):
                    maxima(st, 0)
                    for w in range(2):
                        wait(dve, vh_done, st, 1, 2, w + 1)
                        v.tensor_tensor(vl[64 * w:64 * w + TOK, (e - 1) % 4, :, w::2, 0:HD],
                                        b_ps[64 * w:64 * w + TOK, 0:NP * C].rearrange("p (n h d) -> p h n d", n=NP, d=HD),
                                        vh[64 * w:64 * w + TOK, (e - 1) % 4, :, w::2, 0:HD], ALU.subtract).then_inc(vl_done, 1)
                if real(st, 5):
                    taps(st, (1, 2, 3))
                if real(st, 1):
                    maxima(st, 1)
                if real(st, 6):
                    wait(dve, mlp_done, st, 6)
                    wait_ring(dve, stored, st, 8)
                    v.scalar_tensor_tensor(y[:, (e - 6) % 2, :], d_ps[0:C, 0:CT], b2_c, s2[0:C, (e - 6) % 2, :], ALU.add, ALU.add)\
                     .then_inc(y_done, 1)
                if real(st, 0):
                    wait(dve, rstd_done, st, 0)
                    wait(dve, xl_done, st, 1)
                    v.tensor_tensor(xn[:, :, :].rearrange("c w (r k) -> c w r k", k=WS), image_order(a_ps[0:C, 0:CT], SIDE),
                                    image_order(rstd[:, :], SIDE), ALU.mult).then_inc(xn_done, 1)
                if real(st, 5):
                    taps(st, (4, 5, 6))
                if real(st, 3):
                    normalise(st, 1)
                if real(st, 1):
                    maxima(st, 2)
                if real(st, 5):
                    taps(st, (7, 8))
                if real(st, 3):
                    wait(dve, oh_done, st, 3)
                    v.tensor_tensor(ol[0:C, :, :, :].rearrange("c n a t -> c (n a t)"), a_ps[0:C, :],
                                    oh[0:C, :, :, :].rearrange("c n a t -> c (n a t)"), ALU.subtract).then_inc(ol_done, 1)
                if real(st, 0):
                    for ps, hi, dst, done, out_ in ((b_ps, qh, ql, qh_done, ql_done), (d_ps, kh, kl, kh_done, kl_done)):
                        wait(dve, done, st, 0)
                        v.tensor_tensor(dst[:, e % 2, :].rearrange("c (w t) -> c w t", t=WP)[:, :, 0:TOK],
                                        ps[0:C, 0:CT].rearrange("c (w t) -> c w t", t=TOK),
                                        hi[:, e % 2, :].rearrange("c (w t) -> c w t", t=WP)[:, :, 0:TOK], ALU.subtract).then_inc(out_, 1)
                if real(st, 1):
                    maxima(st, 3)
                if real(st, 3):
                    wait(dve, proj_done, st, 3)
                    _, r = place(st, 3)
                    v.tensor_tensor(image_order(ximg[:, bass.ds(r * CROW + PAD + 1, CROW)], PAD),
                                    a_ps[0:C, 0:CT].rearrange("c (w r k) -> c w r k", w=NW, k=WS),
                                    image_order(x_sb[:, bass.ds(r * CT, CT)], SIDE), ALU.add).then_inc(sum_done, 1)
                if real(st, 1):
                    wait(dve, mxt_done, st, 1)
                    wait_ring(dve, row_in, st, 3)
                    v.tensor_copy(mxt[:, (e - 1) % 2, :], mxt_ps).then_inc(mxt_out, 1)

            run(dve, step)


def kernel(x, L0_conv_ln_g, L0_conv_ln_b, L0_conv_qkv_w, L0_conv_qkv_b, L0_conv_proj_w, L0_conv_proj_b,
           L0_conv_bias_table, L0_conv_conv_w, L0_conv_bn_g, L0_conv_bn_b, L0_conv_bn_mean, L0_conv_bn_var,
           L0_conv_w1, L0_conv_b1, L0_conv_w2, L0_conv_b2):
    import concourse.bacc as bacc
    from concourse.bass_utils import run_bass_kernel_spmd

    def a(v):
        return np.asarray(v)

    order = np.arange(C).reshape(NJ, 2, HD).transpose(1, 2, 0).reshape(-1)
    perm = np.concatenate([order, C + order, 2 * C + np.arange(C)])
    at = np.stack(np.meshgrid(np.arange(WS), np.arange(WS), indexing="ij"), -1).reshape(-1, 2)
    rel = at[:, None] - at[None] + WS - 1
    bias = a(L0_conv_bias_table)[rel[..., 0] * (2 * WS - 1) + rel[..., 1]]
    w_qkv, b_qkv, w_proj = a(L0_conv_qkv_w), a(L0_conv_qkv_b), a(L0_conv_proj_w).T
    col = lambda v: a(v).reshape(C, 1)
    arrays = {
        "x": a(x),
        "w_qkv": w_qkv.T[:, perm],
        "b_qkv_row": b_qkv[perm].reshape(1, -1),
        "b_v": col(b_qkv[2 * C:]),
        "w_proj": w_proj,
        "w_proj2": w_proj.reshape(NJ, 2, HD, C).transpose(1, 0, 2, 3).reshape(2, C // 2, C),
        "b_proj_row": a(L0_conv_proj_b).reshape(1, C),
        "ln_g": col(L0_conv_ln_g), "ln_b": col(L0_conv_ln_b),
        "bias_q": bias.transpose(1, 2, 0).reshape(TOK, -1),
        "bias_k": bias.transpose(0, 2, 1).reshape(TOK, -1),
        "conv_w": a(L0_conv_conv_w).reshape(C, 9),
        "bn_g": col(L0_conv_bn_g), "bn_b": col(L0_conv_bn_b), "bn_mean": col(L0_conv_bn_mean), "bn_var": col(L0_conv_bn_var),
        "w1": a(L0_conv_w1).T, "b1": a(L0_conv_b1).reshape(NB, 128).T,
        "w2": a(L0_conv_w2).T.reshape(NB, 128, C).transpose(1, 0, 2), "b2": col(L0_conv_b2),
        "eye": np.eye(128, dtype=np.float32),
    }
    arrays = {f"in_{k}": np.ascontiguousarray(v) for k, v in arrays.items()}
    nc = bacc.Bacc("TRN2", target_bir_lowering=False, num_devices=1)
    args = [nc.dram_tensor(k, v.shape, mybir.dt.from_np(v.dtype), kind="ExternalInput").ap() for k, v in arrays.items()]
    args.append(nc.dram_tensor("out_0", (BATCH, C, SIDE, SIDE), F32, kind="ExternalOutput").ap())
    block_program(nc, *args)
    r = run_bass_kernel_spmd(nc, [arrays], core_ids=[0])
    return r.results[0]["out_0"]
```

```python
from contextlib import ExitStack

import numpy as np

import concourse.bass as bass
from concourse import mybir

F32, F16 = mybir.dt.float32, mybir.dt.float16
ALU, ACT, AX = mybir.AluOpType, mybir.ActivationFunctionType, mybir.AxisListType

BATCH, C, SIDE, WS, HEADS = 32, 96, 56, 7, 12
HD = C // HEADS
SCALE = HD ** -0.5
HID = 4 * C
NB = HID // 128
EPS = 1e-5
TOK = WS * WS
NW = SIDE // WS
NP = NW // 2
CT = NW * TOK
CPI = SIDE // WS
CHUNKS = BATCH * CPI
WP = 64
NJ = HEADS // 2
ROWS = 64 + TOK
PIECE = 16
VW = HD + 1
PAD = SIDE + 2
CROW = WS * PAD
STEPS = CHUNKS + 8
IMAGE = C * SIDE * SIDE
UN = CPI


def block_program(nc, x, w_qkv, b_qkv_row, b_v, w_proj, w_proj2, b_proj_row, ln_g, ln_b, bias_q, bias_k,
                  conv_w, bn_g, bn_b, bn_mean, bn_var, w1, b1, w2, b2, eye, out):
    ctx = ExitStack()
    with ctx:
        def sb(name, shape, dt=F32):
            return ctx.enter_context(nc.sbuf_tensor(name, shape, dt))

        def sem(name):
            return ctx.enter_context(nc.semaphore(name))

        def sems(name, n):
            return [sem(f"{name}{i}") for i in range(n)]

        wq = sb("wq", [97, 3 * C])
        wp = sb("wp", [97, 4, C])
        wpn_f = sb("wpn_f", [C, C])
        brow = sb("brow", [97, C])
        cols = sb("cols", [C, 24])
        b1_c = sb("b1_c", [128, NB])
        w1_s, w2_s = sb("w1_s", [C, HID]), sb("w2_s", [128, NB, C])
        eye_f, eye_h = sb("eye_f", [128, 128]), sb("eye_h", [128, 128], F16)
        center, avg = sb("center", [C, C]), sb("avg", [C, C])
        lo_l = sb("lo_l", [TOK, HEADS * TOK], F16)
        hot_f, hot_h = sb("hot_f", [ROWS, WP]), sb("hot_h", [ROWS, WP], F16)
        hot2 = sb("hot2", [TOK, 2, WP], F16)
        g_c, b_c, bv_c, bng_c, bnb_c, bnm_c, bnv_c, b2_c = (cols[:, i:i + 1] for i in range(8))
        sc_c, cb_c, bvs_c, eps_c = (cols[:, i:i + 1] for i in range(8, 12))
        cw_c = cols[:, 12:21]
        x_sb = sb("x_sb", [C, CPI * CT])
        sq, rstd = sb("sq", [C, CT]), sb("rstd", [C, CT])
        xn = sb("xn", [97, 2, NW, WP])
        qh, ql, kh, kl = (sb(n, [C, 2, NW * WP], F16) for n in ("qh", "ql", "kh", "kl"))
        k_st = sb("k_st", [ROWS, 4, NJ, NW * WP], F16)
        q_bd = sb("q_bd", [ROWS, 4, HEADS, NW * WP], F16)
        q_st = sb("q_st", [ROWS, 2, NJ, NW * WP], F16)
        k_bd = sb("k_bd", [ROWS, 2, HEADS, NW * WP], F16)
        vh, vl = sb("vh", [128, 4, HEADS, NW, VW], F16), sb("vl", [128, 4, HEADS, NW, VW], F16)
        mx, mxt = sb("mx", [128, 2, HEADS, NP], F16), sb("mxt", [HEADS * NP, 2, 128], F16)
        p32 = sb("p32", [128, 2, HEADS, TOK])
        ph, pl = sb("ph", [128, 2, HEADS, WP], F16), sb("pl", [128, 2, HEADS, WP], F16)
        bias_h = sb("bias_h", [ROWS, 2, HEADS * TOK], F16)
        rec = sb("rec", [128, 2, 2, HEADS])
        on = sb("on", [128, NP, C])
        ot = sb("ot", [97, NP, 2, WP])
        ximg = sb("ximg", [C, PAD * PAD + 4])
        s2 = sb("s2", [97, 2, CT])
        g = sb("g", [128, NB, CT])
        y = sb("y", [97, 2, CT])
        bias_f = p32[0:ROWS, :, :, :].rearrange("p a h t -> p a (h t)")
        lo_f = g[0:TOK, :, :].rearrange("p k t -> p (k t)")[:, 0:HEADS * TOK]
        lo_h = s2[0:TOK, :, :].rearrange("p a t -> p (a t)")[:, 0:HEADS * TOK // 2].bitcast(F16)
        rows_f, wq_f = y[:, 0, 0:3 * C], y[:, 1, 0:3 * C]

        st_ps = ctx.enter_context(nc.psum_tensor("st_ps", [128, 2, 512], F32))
        sm_ps = ctx.enter_context(nc.psum_tensor("sm_ps", [128, 2, 512], F32))
        o_ps = ctx.enter_context(nc.psum_tensor("o_ps", [128, 512], F32))
        a_ps = ctx.enter_context(nc.psum_tensor("a_ps", [128, 512], F32))
        b_ps = ctx.enter_context(nc.psum_tensor("b_ps", [128, 512], F32))
        d_ps = ctx.enter_context(nc.psum_tensor("d_ps", [128, 512], F32))
        mxt_ps = sm_ps[0:HEADS * NP, 0, 0:64].bitcast(F16)
        HALF = NJ // 2 * 2 * TOK

        loaded = sem("loaded")
        dve_setup, act_setup, pe_setup, pool_setup = sem("dve_setup"), sem("act_setup"), sem("pe_setup"), sem("pool_setup")
        ready, shift_done = sem("ready"), sem("shift_done")
        x_in = sems("x_in", 4)
        max_in = sems("max_in", 2)
        exp_in = sems("exp_in", 4)
        row_in = sems("row_in", 2)
        stored = sems("stored", 2)
        xc_done, sq_done, var_done, lnv_done, rstd_done, xn_done = (sem(n) for n in (
            "xc_done", "sq_done", "var_done", "lnv_done", "rstd_done", "xn_done"))
        q_done, k_done, qh_done, kh_done, ql_done, kl_done = (sem(n) for n in (
            "q_done", "k_done", "qh_done", "kh_done", "ql_done", "kl_done"))
        v_done, vh_done, vl_done = sem("v_done"), sem("vh_done"), sem("vl_done")
        sm_done, max_done, mxt_done, mxt_out = sem("sm_done"), sem("max_done"), sem("mxt_done"), sem("mxt_out")
        st_done, p32_done, ph_done, pl_done = sem("st_done"), sem("p32_done"), sem("ph_done"), sem("pl_done")
        pv_done, rec_done, norm_done = sem("pv_done"), sem("rec_done"), sem("norm_done")
        ot_ps_done, ot_done, proj_done, sum_done = (sem(n) for n in ("ot_ps_done", "ot_done", "proj_done", "sum_done"))
        tap0_done, tap_done = sem("tap0_done"), sem("tap_done")
        hid_done, g_done = sem("hid_done"), sem("g_done")
        mlp_done, y_done = sem("mlp_done"), sem("y_done")

        def real(st, lag):
            u, e = st
            return not isinstance(u, int) or 0 <= UN * u + e - lag < CHUNKS

        def wait(eng, s, st, lag, per=1, k=None):
            u, e = st
            v = u * (UN * per) + ((e - lag) * per + (per if k is None else k))
            if not isinstance(v, int) or v > 0:
                eng.wait_ge(s, v)

        def wait_ring(eng, ring, st, lag, per=16):
            u, e = st
            n = len(ring)
            v = u * (UN // n * per) + ((e - lag) // n + 1) * per
            if not isinstance(v, int) or v > 0:
                eng.wait_ge(ring[(e - lag) % n], v)

        def place(st, lag):
            u, e = st
            return u + (e - lag) // UN, (e - lag) % UN

        def dram_place(st, lag):
            u, e = st
            img, r = (e - lag) // UN, (e - lag) % UN
            if isinstance(u, int):
                return (u + img) * IMAGE, 0, r * CT
            return nc.sync.snap((u - 1) * IMAGE), img + 1, r * CT

        def run(eng, step):
            for e in range(UN):
                step((0, e))
            with eng.Fori(1, CHUNKS // UN - 1) as u:
                for e in range(UN):
                    step((u, e))
            for s in range(CHUNKS - UN, STEPS):
                step((s // UN, s % UN))

        def max_pair(p):
            return (1, p - 2) if p >= 2 else (2, p + 2)

        def pv_pair(p):
            return (4, NP - 1) if p == 0 else (3, p - 1)

        def dram_rows(t, at):
            base, img, col = at
            rows = t.rearrange("b c h w -> (b c h w)")[bass.ds(base, (img + 1) * IMAGE)].rearrange("(b c k) -> b c k", b=img + 1, c=C)
            return rows[img, :, col:col + CT]

        def image_order(ap, width):
            return ap.rearrange("c (r w k) -> c w r k", w=NW, k=WS) if width == SIDE else \
                ap.rearrange("c (r q) -> c r q", q=width)[:, :, 0:SIDE].rearrange("c r (w k) -> c w r k", k=WS)

        def image_rows(st, lag, dy, dx):
            at = place(st, lag)[1] * CROW + dy * PAD + dx
            return ximg[:, at:at + CROW].rearrange("c (r q) -> c r q", q=PAD)[:, :, 0:SIDE]

        block = ctx.enter_context(nc.Block())

        @block.sync
        def _(sp):
            loads = [
                (wq_f[0:C, :], w_qkv), (rows_f[96:97, :], b_qkv_row), (brow[96:97, :], b_proj_row),
                (bv_c, b_v), (wpn_f[:, :], w_proj), (g_c, ln_g), (b_c, ln_b), (bng_c, bn_g), (bnb_c, bn_b),
                (bnm_c, bn_mean), (bnv_c, bn_var), (b2_c, b2), (cw_c, conv_w), (b1_c[:, :], b1), (w1_s[:, :], w1),
                (w2_s[:, :, :], w2), (eye_f[:, :], eye),
                (bias_f[64:ROWS, 0, :], bias_q), (bias_f[64:ROWS, 1, :], bias_k), (lo_f, bias_q),
                (hot_f[64:ROWS, :], eye[0:TOK, 0:WP]),
            ]
            sp.wait_ge(pool_setup, 1)
            for w in range(2):
                for h2 in range(2):
                    loads.append((wp[48 * w:48 * w + 48, 2 * w + h2, :], w_proj2[h2]))
            for dst, src in loads:
                sp.dma_start(dst, src).then_inc(loaded, 16)
            sp.wait_ge(loaded, 16 * len(loads))

            def load(c):
                sp.dma_start(x_sb[:, c * CT:(c + 1) * CT], dram_rows(x, (0, 0, c * CT))).then_inc(x_in[c % 4], 16)

            for c in range(2):
                load(c)
            for r in stored:
                sp.sem_inc(r, 16)
            sp.wait_ge(ready, 4)

            def held(v):
                return v if isinstance(v, int) else nc.sync.snap(v)

            def count(st, lag, per=1):
                u, e = st
                return held(u * (UN * per) + (e - lag + 1) * per)

            def wait_for(s, v):
                if not isinstance(v, int) or v > 0:
                    sp.wait_ge(s, v)

            def step(st):
                e = st[1]
                c1, c2, c6, c7 = (count(st, lag) for lag in (1, 2, 6, 7))
                if real(st, -2):
                    at = dram_place(st, -2)
                    wait_for(sum_done, c6)
                    sp.dma_start(x_sb[:, at[2]:at[2] + CT], dram_rows(x, at)).then_inc(x_in[(e + 2) % 4], 16)
                if real(st, 1):
                    r2, r4 = (e - 1) % 2, (e - 1) % 4
                    wait_for(qh_done, c1)
                    sp.dma_start(q_st[16:32, r2, :, :], qh[:, r2, :]).then_inc(max_in[r2], 16)
                    wait_for(kh_done, c1)
                    for h2 in range(2):
                        sp.dma_start(k_bd[16 + 8 * h2:24 + 8 * h2, r2, h2::2, :], kh[48 * h2:48 * h2 + 48, r2, :])\
                          .then_inc(max_in[r2], 16)
                    wait_for(ql_done, c1)
                    wait_for(kl_done, c1)
                    for n, (kk, qq) in enumerate(((kh, qh), (kl, qh), (kh, ql))):
                        r0 = PIECE * (n + 1)
                        sp.dma_start(k_st[r0:r0 + PIECE, r4, :, :], kk[:, r2, :]).then_inc(exp_in[r4], 16)
                        for h2 in range(2):
                            sp.dma_start(q_bd[r0 + 8 * h2:r0 + 8 * h2 + 8, r4, h2::2, :],
                                         qq[48 * h2:48 * h2 + 48, r2, :]).then_inc(exp_in[r4], 16)
                if real(st, 2):
                    wait_for(mxt_out, c2)
                    sp.dma_start(q_bd[0:1, (e - 2) % 4, :, :].rearrange("p h (n c) -> p (h n) c", c=2 * WP),
                                 mxt[:, (e - 2) % 2, :]).then_inc(row_in[(e - 2) % 2], 16)
                if real(st, 7):
                    at = dram_place(st, 7)
                    wait_for(y_done, c7)
                    sp.dma_start(dram_rows(out, at),
                                 y[0:C, (e - 7) % 2, :]).then_inc(stored[(e - 7) % 2], 16)

            run(sp, step)
            for r in stored:
                sp.wait_ge(r, 16 * (CHUNKS // 2 + 1))

        @block.tensor
        def _(pe):
            mm = nc.tensor.matmul

            def three(o, sh, sl, mh, ml, start=True, stop=True):
                mm(o, sh, mh, start=start, stop=False)
                mm(o, sh, ml, start=False, stop=False)
                return mm(o, sl, mh, start=False, stop=stop)

            pe.wait_ge(loaded, 16 * 25)
            mm(a_ps[96:97, 0:3 * C], b_c, wq_f[0:C, :], start=True, stop=True)
            mm(b_ps[0:C, 0:1], wq_f[0:C, 2 * C:], b_c, start=True, stop=True).then_inc(pe_setup, 1)
            pe.wait_ge(dve_setup, 2)
            mm(d_ps[96:97, 0:C], bvs_c, wpn_f[:, :], start=True, stop=True).then_inc(pe_setup, 1)
            pe.wait_ge(shift_done, 1)
            for k in range(NB):
                last = mm(st_ps[:, 0, k:k + 1], w1_s[:, k * 128:(k + 1) * 128], cb_c, start=True, stop=True)
            last.then_inc(pe_setup, 1)
            pe.wait_ge(ready, 4)

            def exp_scores(st, q):
                r = (st[1] - 3) % 4
                if q == 0:
                    wait_ring(pe, exp_in, st, 3, 9 * 16)
                    wait_ring(pe, row_in, st, 3)
                wait(pe, ph_done, st, 3, NP, q)
                for b in range(2):
                    mm(st_ps[:, b, 0:HALF], hot2[:, :, :].rearrange("p a b -> p (a b)"), lo_l[:, b * HALF:(b + 1) * HALF],
                       start=True, stop=False, skip_group_check=True)
                for j in range(NJ):
                    for w in range(2):
                        n = (2 * q + w) * WP
                        c0 = j % (NJ // 2) * 2 * TOK
                        last = mm(st_ps[64 * w:64 * w + 64, j // (NJ // 2), c0:c0 + 2 * TOK], k_st[:, r, j, n:n + WP],
                                  q_bd[:, r, 2 * j:2 * j + 2, n:n + TOK], start=False, stop=True, skip_group_check=True)
                last.then_inc(st_done, 1)

            def max_scores(st, lag, p):
                if p == 0:
                    wait_ring(pe, max_in, st, lag, 3 * 16)
                    wait(pe, mxt_out, st, lag + 1)
                wait(pe, max_done, st, lag, NP, p)
                r = (st[1] - lag) % 2
                for j in range(NJ):
                    for w in range(2):
                        n = (2 * p + w) * WP
                        c0 = j % (NJ // 2) * 2 * TOK
                        last = mm(sm_ps[64 * w:64 * w + 64, j // (NJ // 2), c0:c0 + 2 * TOK], q_st[:, r, j, n:n + WP],
                                  k_bd[:, r, 2 * j:2 * j + 2, n:n + TOK], start=True, stop=True)
                last.then_inc(sm_done, 1)

            def values_times_p(st, lag, q):
                if q == 0:
                    wait(pe, vl_done, st, lag, 2)
                wait(pe, pl_done, st, lag, NP, q + 1)
                if q % 2 == 0:
                    wait(pe, norm_done, st, lag, 4, q)
                r, r2 = (st[1] - lag) % 4, q % 2
                for j in range(NJ):
                    o = o_ps[:, r2 * 256:r2 * 256 + 2 * HEADS * VW].rearrange("p (w h) -> p w h", w=2)[:, :, j * 2 * VW:(j + 1) * 2 * VW]

                    def moving(v):
                        return v[:, r, 2 * j:2 * j + 2, 2 * q:2 * q + 2, :].rearrange("p h w d -> p w h d")

                    s_h = ph[:, r2, 2 * j:2 * j + 2, :].rearrange("p h n -> p (h n)")
                    s_l = pl[:, r2, 2 * j:2 * j + 2, :].rearrange("p h n -> p (h n)")
                    last = three(o, s_h, s_l, moving(vh), moving(vl))
                last.then_inc(pv_done, 1)

            def centred(st):
                wait_ring(pe, x_in, st, 0)
                wait(pe, sum_done, st, 5)
                _, r = place(st, 0)
                mm(a_ps[0:C, 0:CT], center[:, :], x_sb[:, r * CT:(r + 1) * CT], start=True, stop=True).then_inc(xc_done, 1)

            def variance(st):
                wait(pe, sq_done, st, 0)
                wait(pe, g_done, st, 7, NB, 2)
                if real(st, 1) and not real(st, 7):
                    wait(pe, ql_done, st, 1)
                mm(d_ps[0:C, 0:CT], avg[:, :], sq[:, :], start=True, stop=True).then_inc(var_done, 1)

            def q_and_k(st):
                wait(pe, xn_done, st, 0)
                m = xn[:, st[1] % 2, :, 0:TOK]
                wait(pe, vl_done, st, 1, 2)
                mm(d_ps[0:C, 0:CT], wq[:, 0:C], m, start=True, stop=True).then_inc(q_done, 1)
                wait(pe, ot_done, st, 4)
                mm(b_ps[0:C, 0:CT], wq[:, C:2 * C], m, start=True, stop=True).then_inc(k_done, 1)

            def values(st):
                wait(pe, rstd_done, st, 0) if real(st, 0) else None
                for n in range(NP):
                    last = mm(d_ps[:, n * C:(n + 1) * C], xn[0:C, (st[1] - 1) % 2, 2 * n:2 * n + 2, :].rearrange("c w n -> c (w n)"),
                              wq[0:C, 2 * C:], start=True, stop=True)
                last.then_inc(v_done, 1)

            def channels_first(st):
                wait(pe, norm_done, st, 4, 4)
                wait(pe, y_done, st, 7)
                if real(st, 1) and not real(st, 7):
                    wait(pe, kl_done, st, 1)
                for n in range(NP):
                    last = nc.tensor.transpose(b_ps[0:C, n * 128:(n + 1) * 128], on[:, n, :], eye_f[:, :])
                last.then_inc(ot_ps_done, 1)

            def projection(st):
                wait(pe, ot_done, st, 4)
                if real(st, 0):
                    wait(pe, xn_done, st, 0)
                for w in range(2):
                    o = a_ps[0:C, 0:CT].rearrange("c (n w t) -> c w n t", w=2, t=TOK)[:, w]
                    for h2 in range(2):
                        last = mm(o, wp[:, 2 * w + h2, :], ot[:, :, h2, 0:TOK], start=h2 == 0, stop=h2 == 1)
                last.then_inc(proj_done, 1)

            def hidden(st):
                wait(pe, tap_done, st, 7, 8)
                if real(st, 1):
                    wait(pe, kl_done, st, 1)
                for k in range(NB):
                    if k == 1 and real(st, 1):
                        wait(pe, ql_done, st, 1)
                    if k == 2:
                        wait(pe, g_done, st, 7, NB, 1)
                    t = b_ps if k % 2 == 0 else d_ps
                    mm(t[:, 0:CT], w1_s[:, k * 128:(k + 1) * 128], s2[0:C, (st[1] - 7) % 2, :], start=True, stop=True)\
                        .then_inc(hid_done, 1)

            def second(st):
                wait(pe, g_done, st, 7, NB)
                for k in range(NB):
                    last = mm(b_ps[0:C, 0:CT], w2_s[:, k, :], g[:, k, :], start=k == 0, stop=k == NB - 1)
                last.then_inc(mlp_done, 1)

            def maxima_rows(st):
                nc.tensor.transpose(mxt_ps, mx[:, (st[1] - 2) % 2, :, :].rearrange("p h n -> p (h n)"), eye_h[:, :])\
                  .then_inc(mxt_done, 1)

            def step(st):
                def exp_and_max(p):
                    if real(st, 3):
                        exp_scores(st, p)
                    lag, q = max_pair(p)
                    if real(st, lag):
                        max_scores(st, lag, q)

                def pv(p):
                    lag, q = pv_pair(p)
                    if real(st, lag):
                        values_times_p(st, lag, q)

                exp_and_max(0)
                pv(0)
                if real(st, 0):
                    centred(st)
                if real(st, 7):
                    hidden(st)
                exp_and_max(1)
                if real(st, 0):
                    variance(st)
                if real(st, 2):
                    wait(pe, max_done, st, 2, NP)
                if real(st, 7):
                    second(st)
                if real(st, 2):
                    maxima_rows(st)
                pv(1)
                if real(st, 3):
                    exp_scores(st, 2)
                if real(st, 1):
                    values(st)
                    max_scores(st, 1, 0)
                if real(st, 4):
                    channels_first(st)
                pv(2)
                exp_and_max(3)
                if real(st, 0):
                    q_and_k(st)
                if real(st, 4):
                    projection(st)
                pv(3)

            run(pe, step)

        @block.scalar
        def _(act):
            af = nc.scalar.activation
            act.preload_act_table_set("natural_log_exp_and_others")
            act.wait_ge(loaded, 16 * 25)
            act.wait_ge(dve_setup, 1)
            af(sc_c, bnv_c, ACT.Ln, bias=eps_c).then_inc(act_setup, 1)
            act.wait_ge(act_setup, 1)
            af(sc_c, sc_c, ACT.Exp, scale=-0.5).then_inc(act_setup, 1)
            act.wait_ge(ready, 4)

            def exps(st, q):
                wait(act, st_done, st, 3, NP, q + 1)
                wait(act, pl_done, st, 3, NP, q - 1)
                src = st_ps[:, :, 0:HALF].rearrange("p b (h n) -> p b h n", n=TOK)
                af(p32[:, q % 2, :, :].rearrange("p (b h) n -> p b h n", b=2), src, ACT.Exp).then_inc(p32_done, 1)
                wait(act, pv_done, st, 3, NP, q - 1)
                af(ph[:, q % 2, :, 0:TOK].rearrange("p (b h) n -> p b h n", b=2), src, ACT.Exp).then_inc(ph_done, 1)

            def step(st):
                e = st[1]
                if real(st, 3):
                    exps(st, 0)
                if real(st, 1):
                    wait_ring(act, exp_in, st, 3, 9 * 16)
                    wait_ring(act, max_in, st, 3, 3 * 16)
                    for ps, dst, done, out_ in ((d_ps, qh, q_done, qh_done), (b_ps, kh, k_done, kh_done)):
                        wait(act, done, st, 1)
                        af(dst[:, (e - 1) % 2, :].rearrange("c (w t) -> c w t", t=WP)[:, :, 0:TOK],
                           ps[0:C, 0:CT].rearrange("c (w t) -> c w t", t=TOK), ACT.Identity).then_inc(out_, 1)
                if real(st, 0):
                    wait(act, xc_done, st, 0)
                    wait(act, var_done, st, 1)
                    af(sq[:, :], a_ps[0:C, 0:CT], ACT.Square).then_inc(sq_done, 1)
                if real(st, 7):
                    wait(act, mlp_done, st, 8)
                    for k in range(NB):
                        t = b_ps if k % 2 == 0 else d_ps
                        wait(act, hid_done, st, 7, NB, k + 1)
                        af(g[:, k, :], t[:, 0:CT], ACT.Gelu, bias=b1_c[:, k:k + 1]).then_inc(g_done, 1)
                    act.preload_act_table_set("natural_log_exp_and_others")
                if real(st, 3):
                    exps(st, 1)
                if real(st, 0):
                    wait(act, var_done, st, 0)
                    wait(act, xn_done, st, 1)
                    af(rstd[:, :], d_ps[0:C, 0:CT], ACT.Ln, bias=eps_c).then_inc(lnv_done, 1)
                    wait(act, lnv_done, st, 0)
                    af(rstd[:, :], rstd[:, :], ACT.Exp, scale=-0.5).then_inc(rstd_done, 1)
                if real(st, 3):
                    exps(st, 2)
                if real(st, 1):
                    wait(act, v_done, st, 1)
                    wait(act, pv_done, st, 5, NP)
                    for w in range(2):
                        af(vh[64 * w:64 * w + TOK, (e - 1) % 4, :, w::2, 0:HD],
                           d_ps[64 * w:64 * w + TOK, 0:NP * C].rearrange("p (n h d) -> p h n d", n=NP, d=HD),
                           ACT.Identity).then_inc(vh_done, 1)
                if real(st, 4):
                    wait(act, ot_ps_done, st, 4)
                    wait(act, proj_done, st, 5)
                    af(ot[0:C, :, :, :].rearrange("c n a t -> c (n a t)"), b_ps[0:C, :], ACT.Identity).then_inc(ot_done, 1)
                if real(st, 3):
                    exps(st, 3)

            run(act, step)

        @block.gpsimd
        def _(pool):
            tt = nc.gpsimd.tensor_tensor
            nc.gpsimd.memset(wp[:, :, :], 0.0).then_inc(pool_setup, 1)
            for t in (q_bd, xn, ot, qh, ql, kh, kl, ph, pl, on):
                nc.gpsimd.memset(t[:], 0.0)
            nc.gpsimd.memset(ximg[:, :], 0.0).then_inc(pool_setup, 1)
            pool.wait_ge(pool_setup, 2)
            nc.gpsimd.memset(xn[96:97, :, :, :], 1.0)
            nc.gpsimd.memset(ot[96:97, :, :, :], 1.0).then_inc(pool_setup, 1)
            pool.wait_ge(pool_setup, 3)
            pool.sem_inc(ready, 1)
            pool.wait_ge(ready, 4)

            def step(st):
                e = st[1]
                for p in range(NP):
                    if real(st, 3):
                        wait(pool, ph_done, st, 3, NP, p + 1)
                        wait(pool, pv_done, st, 3, NP, p - 1)
                        tt(pl[:, p % 2, :, 0:TOK], p32[:, p % 2, :, :], ph[:, p % 2, :, 0:TOK], ALU.subtract).then_inc(pl_done, 1)
                    if p == 0 and real(st, 6):
                        if real(st, 5):
                            wait(pool, sum_done, st, 5)
                        wait(pool, y_done, st, 8)
                        tt(s2[0:C, e % 2, :].rearrange("c (r q) -> c r q", q=SIDE), image_rows(st, 6, 0, 0),
                           cw_c[:, 0:1].unsqueeze(2).broadcast_to([C, WS, SIDE]), ALU.mult).then_inc(tap0_done, 1)

            run(pool, step)

        @block.vector
        def _(dve):
            v = nc.vector
            at = [0]

            def link(ins):
                at[0] += 1
                ins.then_inc(dve_setup, 1)
                dve.wait_ge(dve_setup, at[0])

            link(v.memset(eps_c, EPS))
            dve.wait_ge(loaded, 16 * 25)
            dve.wait_ge(pe_setup, 1)
            link(v.tensor_tensor(bvs_c, b_ps[0:C, 0:1], bv_c, ALU.add))
            link(v.tensor_scalar(wq[0:C, :], wq_f[0:C, :], g_c, None, ALU.mult))
            link(v.tensor_tensor(wq[96:97, :], a_ps[96:97, 0:3 * C], rows_f[96:97, :], ALU.add))
            link(v.tensor_scalar(wq[:, 0:C], wq[:, 0:C], SCALE, None, ALU.mult))
            dve.wait_ge(pe_setup, 2)
            for w in range(2):
                link(v.tensor_tensor(wp[96:97, 2 * w, :], d_ps[96:97, 0:C], brow[96:97, :], ALU.add))
            link(v.memset(hot2[:, :, :], 0.0))
            for w in range(2):
                link(v.tensor_copy(hot2[:, w, 0:TOK], eye_f[0:TOK, 0:TOK]))
            link(v.tensor_copy(lo_h, lo_f))
            link(v.tensor_tensor(lo_l[:, :], lo_f, lo_h, ALU.subtract))
            link(v.tensor_copy(eye_h[:, :], eye_f[:, :]))
            link(v.tensor_scalar(center[:, :], eye_f[0:C, 0:C], -1.0 / C, None, ALU.add))
            link(v.memset(avg[:, :], 1.0 / C))
            dve.wait_ge(act_setup, 2)
            link(v.tensor_tensor(sc_c, sc_c, bng_c, ALU.mult))
            link(v.tensor_scalar(cw_c, cw_c, sc_c, None, ALU.mult))
            link(v.tensor_tensor(cb_c, bnm_c, sc_c, ALU.mult))
            link(v.tensor_tensor(cb_c, bnb_c, cb_c, ALU.subtract))
            dve.sem_inc(shift_done, 1)
            link(v.tensor_tensor(b2_c, b2_c, cb_c, ALU.add))
            dve.wait_ge(pe_setup, 3)
            link(v.tensor_tensor(b1_c[:, :], b1_c[:, :], st_ps[:, 0, 0:NB], ALU.add))
            for t in (q_st, k_st, k_bd, vh, vl):
                link(v.memset(t[:], 0.0))
            dve.wait_ge(pool_setup, 3)
            link(v.tensor_copy(hot_h[64:ROWS, :], hot_f[64:ROWS, :]))
            link(v.tensor_copy(bias_h[64:ROWS, :, :], bias_f[64:ROWS, :, :]))
            for r in range(4):
                for t, n, which in ((k_st, 4, None), (q_st, 2, None), (q_bd, 4, 0), (k_bd, 2, 1)):
                    if r >= n:
                        continue
                    if which is None:
                        link(v.tensor_copy(t[64:ROWS, r, :, :].rearrange("p j (w t) -> p (j w) t", t=WP),
                                           hot_h[64:ROWS, :].unsqueeze(1).broadcast_to([TOK, NJ * NW, WP])))
                    else:
                        link(v.tensor_copy(t[64:ROWS, r, :, :].rearrange("p h (w t) -> p h w t", t=WP)[:, :, :, 0:TOK],
                                           bias_h[64:ROWS, which, :].rearrange("p (h t) -> p h t", t=TOK)
                                           .unsqueeze(2).broadcast_to([TOK, HEADS, NW, TOK])))
                link(v.memset(k_st[0:1, r, :, :].rearrange("p j (w t) -> p (j w) t", t=WP)[:, :, 0:TOK], -1.0))
                for w in range(2):
                    link(v.memset(vh[64 * w:64 * w + TOK, r, :, w::2, HD:VW], 1.0))
            dve.sem_inc(ready, 3)

            def maxima(st, slot):
                lag, p = max_pair(slot)
                if not real(st, lag):
                    return
                wait(dve, sm_done, st, lag, NP, p + 1)
                wait(dve, mxt_done, st, lag + 2)
                v.tensor_reduce(mx[:, (st[1] - lag) % 2, :, p].rearrange("p (b h) -> p b h", b=2),
                                sm_ps[:, :, 0:HALF].rearrange("p b (h n) -> p b h n", n=TOK), AX.X, ALU.max)\
                 .then_inc(max_done, 1)

            def normalise(st, lag, half):
                if not real(st, lag):
                    return
                wait(dve, pv_done, st, lag, NP, 2 * half + 2)
                wait(dve, ot_ps_done, st, lag + 1)
                o = o_ps[:, :].rearrange("p (n c) -> p n c", n=2)[:, :, 0:2 * HEADS * VW].rearrange("p n (g a d) -> p n g a d", a=2, d=VW)
                for h2 in range(2):
                    rows = slice(64 * h2, 64 * h2 + TOK)
                    v.reciprocal(rec[rows, half, :, :], o[rows, :, :, h2, HD]).then_inc(rec_done, 1)
                for h2 in range(2):
                    rows = slice(64 * h2, 64 * h2 + TOK)
                    wait(dve, rec_done, st, lag, 4, 2 * half + h2 + 1)
                    v.tensor_tensor(on[rows, 2 * half:2 * half + 2, :].rearrange("p n (g d) -> p n g d", d=HD),
                                    o[rows, :, :, h2, 0:HD], rec[rows, half, :, :].unsqueeze(3).broadcast_to([TOK, 2, HEADS, HD]),
                                    ALU.mult).then_inc(norm_done, 1)

            def tap(st, k):
                if not real(st, 6):
                    return
                acc = s2[0:C, st[1] % 2, :].rearrange("c (r q) -> c r q", q=SIDE)
                if k == 1:
                    wait(dve, tap0_done, st, 6)
                else:
                    wait(dve, tap_done, st, 6, 8, k - 1)
                v.scalar_tensor_tensor(acc, image_rows(st, 6, k // 3, k % 3), cw_c[:, k:k + 1], acc, ALU.mult, ALU.add)\
                 .then_inc(tap_done, 1)

            def step(st):
                e = st[1]
                if real(st, 5):
                    wait(dve, proj_done, st, 5)
                    r = place(st, 5)[1]
                    at = r * CROW + PAD + 1
                    v.tensor_tensor(image_order(ximg[:, at:at + CROW], PAD),
                                    a_ps[0:C, 0:CT].rearrange("c (w r k) -> c w r k", w=NW, k=WS),
                                    image_order(x_sb[:, r * CT:(r + 1) * CT], SIDE), ALU.add).then_inc(sum_done, 1)
                maxima(st, 0)
                if real(st, 1):
                    for ps, hi, dst, done, out_ in ((d_ps, qh, ql, qh_done, ql_done), (b_ps, kh, kl, kh_done, kl_done)):
                        wait(dve, done, st, 1)
                        v.tensor_tensor(dst[:, (e - 1) % 2, :].rearrange("c (w t) -> c w t", t=WP)[:, :, 0:TOK],
                                        ps[0:C, 0:CT].rearrange("c (w t) -> c w t", t=TOK),
                                        hi[:, (e - 1) % 2, :].rearrange("c (w t) -> c w t", t=WP)[:, :, 0:TOK], ALU.subtract).then_inc(out_, 1)
                normalise(st, 4, 1)
                tap(st, 1)
                maxima(st, 1)
                tap(st, 2)
                if real(st, 2):
                    wait(dve, mxt_done, st, 2)
                    wait_ring(dve, row_in, st, 4)
                    v.tensor_copy(mxt[:, (e - 2) % 2, :], mxt_ps).then_inc(mxt_out, 1)
                if real(st, 0):
                    wait(dve, rstd_done, st, 0)
                    wait(dve, v_done, st, 2)
                    v.tensor_tensor(xn[0:C, e % 2, :, 0:TOK].rearrange("c w (r k) -> c w r k", k=WS), image_order(a_ps[0:C, 0:CT], SIDE),
                                    image_order(rstd[:, :], SIDE), ALU.mult).then_inc(xn_done, 1)
                tap(st, 3)
                if real(st, 7):
                    wait(dve, mlp_done, st, 7)
                    wait_ring(dve, stored, st, 7)
                    v.scalar_tensor_tensor(y[0:C, (e - 7) % 2, :], b_ps[0:C, 0:CT], b2_c, s2[0:C, (e - 7) % 2, :], ALU.add, ALU.add)\
                     .then_inc(y_done, 1)
                tap(st, 4)
                maxima(st, 2)
                tap(st, 5)
                if real(st, 1):
                    for w in range(2):
                        wait(dve, vh_done, st, 1, 2, w + 1)
                        v.tensor_tensor(vl[64 * w:64 * w + TOK, (e - 1) % 4, :, w::2, 0:HD],
                                        d_ps[64 * w:64 * w + TOK, 0:NP * C].rearrange("p (n h d) -> p h n d", n=NP, d=HD),
                                        vh[64 * w:64 * w + TOK, (e - 1) % 4, :, w::2, 0:HD], ALU.subtract).then_inc(vl_done, 1)
                tap(st, 6)
                normalise(st, 3, 0)
                tap(st, 7)
                maxima(st, 3)
                tap(st, 8)

            run(dve, step)


def kernel(x, L0_conv_ln_g, L0_conv_ln_b, L0_conv_qkv_w, L0_conv_qkv_b, L0_conv_proj_w, L0_conv_proj_b,
           L0_conv_bias_table, L0_conv_conv_w, L0_conv_bn_g, L0_conv_bn_b, L0_conv_bn_mean, L0_conv_bn_var,
           L0_conv_w1, L0_conv_b1, L0_conv_w2, L0_conv_b2):
    import concourse.bacc as bacc
    from concourse.bass_utils import run_bass_kernel_spmd

    def a(v):
        return np.asarray(v)

    order = np.arange(C).reshape(NJ, 2, HD).transpose(1, 2, 0).reshape(-1)
    perm = np.concatenate([order, C + order, 2 * C + np.arange(C)])
    at = np.stack(np.meshgrid(np.arange(WS), np.arange(WS), indexing="ij"), -1).reshape(-1, 2)
    rel = at[:, None] - at[None] + WS - 1
    bias = a(L0_conv_bias_table)[rel[..., 0] * (2 * WS - 1) + rel[..., 1]]
    w_qkv, b_qkv, w_proj = a(L0_conv_qkv_w), a(L0_conv_qkv_b), a(L0_conv_proj_w).T
    col = lambda v: a(v).reshape(C, 1)
    arrays = {
        "x": a(x),
        "w_qkv": w_qkv.T[:, perm],
        "b_qkv_row": b_qkv[perm].reshape(1, -1),
        "b_v": col(b_qkv[2 * C:]),
        "w_proj": w_proj,
        "w_proj2": w_proj.reshape(NJ, 2, HD, C).transpose(1, 0, 2, 3).reshape(2, C // 2, C),
        "b_proj_row": a(L0_conv_proj_b).reshape(1, C),
        "ln_g": col(L0_conv_ln_g), "ln_b": col(L0_conv_ln_b),
        "bias_q": bias.transpose(1, 2, 0).reshape(TOK, -1),
        "bias_k": bias.transpose(0, 2, 1).reshape(TOK, -1),
        "conv_w": a(L0_conv_conv_w).reshape(C, 9),
        "bn_g": col(L0_conv_bn_g), "bn_b": col(L0_conv_bn_b), "bn_mean": col(L0_conv_bn_mean), "bn_var": col(L0_conv_bn_var),
        "w1": a(L0_conv_w1).T, "b1": a(L0_conv_b1).reshape(NB, 128).T,
        "w2": a(L0_conv_w2).T.reshape(NB, 128, C).transpose(1, 0, 2), "b2": col(L0_conv_b2),
        "eye": np.eye(128, dtype=np.float32),
    }
    arrays = {f"in_{k}": np.ascontiguousarray(v) for k, v in arrays.items()}
    nc = bacc.Bacc("TRN2", target_bir_lowering=False, num_devices=1)
    args = [nc.dram_tensor(k, v.shape, mybir.dt.from_np(v.dtype), kind="ExternalInput").ap() for k, v in arrays.items()]
    args.append(nc.dram_tensor("out_0", (BATCH, C, SIDE, SIDE), F32, kind="ExternalOutput").ap())
    block_program(nc, *args)
    r = run_bass_kernel_spmd(nc, [arrays], core_ids=[0])
    return r.results[0]["out_0"]
```

```python
from contextlib import ExitStack

import numpy as np

import concourse.bass as bass
from concourse import mybir

F32, F16 = mybir.dt.float32, mybir.dt.float16
ALU, ACT, AX = mybir.AluOpType, mybir.ActivationFunctionType, mybir.AxisListType

BATCH, C, SIDE, WS, HEADS = 32, 96, 56, 7, 12
HD = C // HEADS
SCALE = HD ** -0.5
HID = 4 * C
NB = HID // 128
EPS = 1e-5
TOK = WS * WS
NW = SIDE // WS
NP = NW // 2
CT = NW * TOK
CPI = SIDE // WS
CHUNKS = BATCH * CPI
WP = 64
NJ = HEADS // 2
ROWS = 64 + TOK
PIECE = 16
VW = HD + 1
PAD = SIDE + 2
CROW = WS * PAD
STEPS = CHUNKS + 8
IMAGE = C * SIDE * SIDE
UP = 256.0
LOADS = 25
UN = CPI


def block_program(nc, x, w_qkv, b_qkv_row, b_v, w_proj, w_proj2, b_proj_row, ln_g, ln_b, bias_q, bias_k,
                  conv_w, bn_g, bn_b, bn_mean, bn_var, w1, b1, w2, b2, eye, out):
    ctx = ExitStack()
    with ctx:
        def sb(name, shape, dt=F32):
            return ctx.enter_context(nc.sbuf_tensor(name, shape, dt))

        def sem(name):
            return ctx.enter_context(nc.semaphore(name))

        def sems(name, n):
            return [sem(f"{name}{i}") for i in range(n)]

        wq_h, wq_l = sb("wq_h", [97, 3 * C], F16), sb("wq_l", [97, 3 * C], F16)
        wp_h, wp_l = sb("wp_h", [97, 4, C], F16), sb("wp_l", [97, 4, C], F16)
        wp = sb("wp", [97, 4, C])
        wpn_f = sb("wpn_f", [C, C])
        brow = sb("brow", [97, C])
        cols = sb("cols", [C, 24])
        b1_c = sb("b1_c", [128, NB])
        w1_s, w2_s = sb("w1_s", [C, HID]), sb("w2_s", [128, NB, C])
        eye_f, eye_h = sb("eye_f", [128, 128]), sb("eye_h", [128, 128], F16)
        center, avg = sb("center", [C, C]), sb("avg", [C, C])
        lo_l = sb("lo_l", [TOK, HEADS * TOK], F16)
        hot_f, hot_h = sb("hot_f", [ROWS, WP]), sb("hot_h", [ROWS, WP], F16)
        hot2 = sb("hot2", [TOK, 2, WP], F16)
        minus = sb("minus", [1, WP], F16)
        g_c, b_c, bv_c, bng_c, bnb_c, bnm_c, bnv_c, b2_c = (cols[:, i:i + 1] for i in range(8))
        sc_c, cb_c, bvs_c, eps_c = (cols[:, i:i + 1] for i in range(8, 12))
        cw_c = cols[:, 12:21]
        x_sb = sb("x_sb", [C, CPI * CT])
        sq, rstd = sb("sq", [C, CT]), sb("rstd", [C, CT])
        xn = sb("xn", [C, NW, TOK])
        xh, xl = sb("xh", [97, 2, NW, WP], F16), sb("xl", [97, 2, NW, WP], F16)
        qh, ql, kh, kl = (sb(n, [C, 2, NW * WP], F16) for n in ("qh", "ql", "kh", "kl"))
        qm = sb("qm", [C, 2, 2 * (NW + 1) * WP], F16)
        k_st = sb("k_st", [ROWS, 4, NJ, NW * WP], F16)
        q_bd = sb("q_bd", [ROWS, 4, HEADS, NW * WP], F16)
        q_st = sb("q_st", [ROWS, 2, NJ, NW * WP], F16)
        k_bd = sb("k_bd", [ROWS, 2, HEADS, NW * WP], F16)
        vh, vl = sb("vh", [128, 4, HEADS, NW, VW], F16), sb("vl", [128, 4, HEADS, NW, VW], F16)
        mx, mxt = sb("mx", [128, 2, HEADS, NP], F16), sb("mxt", [HEADS * NP, 2, 128], F16)
        p32 = sb("p32", [128, 2, HEADS, TOK])
        ph, pl = sb("ph", [128, 2, HEADS, WP], F16), sb("pl", [128, 2, HEADS, WP], F16)
        bias_h = sb("bias_h", [ROWS, 2, HEADS * TOK], F16)
        rec = sb("rec", [128, 2, 2, HEADS])
        on = sb("on", [128, NP, C])
        oh, ol = sb("oh", [97, NP, 2, WP], F16), sb("ol", [97, NP, 2, WP], F16)
        ximg = sb("ximg", [C, PAD * PAD + 4])
        s2 = sb("s2", [97, 2, CT])
        g = sb("g", [128, NB, CT])
        y = sb("y", [97, 2, CT])
        bias_f = p32[0:ROWS, :, :, :].rearrange("p a h t -> p a (h t)")
        lo_f = g[0:TOK, :, :].rearrange("p k t -> p (k t)")[:, 0:HEADS * TOK]
        lo_h = s2[0:TOK, :, :].rearrange("p a t -> p (a t)")[:, 0:HEADS * TOK // 2].bitcast(F16)
        rows_f, wq_f = y[:, 0, 0:3 * C], y[:, 1, 0:3 * C]
        wq = g[0:97, 2, 0:3 * C]

        st_ps = ctx.enter_context(nc.psum_tensor("st_ps", [128, 2, 512], F32))
        sm_ps = ctx.enter_context(nc.psum_tensor("sm_ps", [128, 2, 512], F32))
        o_ps = ctx.enter_context(nc.psum_tensor("o_ps", [128, 512], F32))
        a_ps = ctx.enter_context(nc.psum_tensor("a_ps", [128, 512], F32))
        b_ps = ctx.enter_context(nc.psum_tensor("b_ps", [128, 512], F32))
        d_ps = ctx.enter_context(nc.psum_tensor("d_ps", [128, 512], F32))
        mxt_ps = sm_ps[0:HEADS * NP, 0, 0:64].bitcast(F16)
        HALF = NJ // 2 * 2 * TOK

        loaded = sem("loaded")
        dve_setup, act_setup, pe_setup, pool_setup = sem("dve_setup"), sem("act_setup"), sem("pe_setup"), sem("pool_setup")
        ready, shift_done = sem("ready"), sem("shift_done")
        x_in = sems("x_in", 4)
        max_in = sems("max_in", 2)
        exp_in = sems("exp_in", 4)
        row_in = sems("row_in", 2)
        stored = sems("stored", 2)
        xc_done, sq_done, var_done, lnv_done, rstd_done, xn_done = (sem(n) for n in (
            "xc_done", "sq_done", "var_done", "lnv_done", "rstd_done", "xn_done"))
        xh_done, xl_done = sem("xh_done"), sem("xl_done")
        q_done, k_done, qh_done, kh_done, ql_done, kl_done = (sem(n) for n in (
            "q_done", "k_done", "qh_done", "kh_done", "ql_done", "kl_done"))
        qm_done = sem("qm_done")
        v_done, vh_done, vl_done = sem("v_done"), sem("vh_done"), sem("vl_done")
        sm_done, max_done, mxt_done, mxt_out = sem("sm_done"), sem("max_done"), sem("mxt_done"), sem("mxt_out")
        st_done, ph_done, pl_done = sem("st_done"), sem("ph_done"), sem("pl_done")
        pv_done, rec_done, norm_done = sem("pv_done"), sem("rec_done"), sem("norm_done")
        ot_ps_done, oh_done, ol_done, proj_done, sum_done = (sem(n) for n in ("ot_ps_done", "oh_done", "ol_done", "proj_done", "sum_done"))
        tap0_done, tap_done = sem("tap0_done"), sem("tap_done")
        hid_done, g_done = sem("hid_done"), sem("g_done")
        mlp_done, y_done = sem("mlp_done"), sem("y_done")

        def real(st, lag):
            u, e = st
            return not isinstance(u, int) or 0 <= UN * u + e - lag < CHUNKS

        def wait(eng, s, st, lag, per=1, k=None):
            u, e = st
            v = u * (UN * per) + ((e - lag) * per + (per if k is None else k))
            if not isinstance(v, int) or v > 0:
                eng.wait_ge(s, v)

        def wait_ring(eng, ring, st, lag, per=16):
            u, e = st
            n = len(ring)
            v = u * (UN // n * per) + ((e - lag) // n + 1) * per
            if not isinstance(v, int) or v > 0:
                eng.wait_ge(ring[(e - lag) % n], v)

        def place(st, lag):
            u, e = st
            return u + (e - lag) // UN, (e - lag) % UN

        def dram_place(st, lag):
            u, e = st
            img, r = (e - lag) // UN, (e - lag) % UN
            if isinstance(u, int):
                return (u + img) * IMAGE, 0, r * CT
            return nc.sync.snap((u - 1) * IMAGE), img + 1, r * CT

        def run(eng, step):
            for e in range(UN):
                step((0, e))
            with eng.Fori(1, CHUNKS // UN - 1) as u:
                for e in range(UN):
                    step((u, e))
            for s in range(CHUNKS - UN, STEPS):
                step((s // UN, s % UN))

        def dram_rows(t, at):
            base, img, col = at
            rows = t.rearrange("b c h w -> (b c h w)")[bass.ds(base, (img + 1) * IMAGE)].rearrange("(b c k) -> b c k", b=img + 1, c=C)
            return rows[img, :, col:col + CT]

        def words(ap):
            dims = " ".join("abcdefgh"[:len(ap.shape) - 1])
            flat = ap.rearrange(f"p {dims} -> p ({dims})")
            return flat if ap.dtype == F32 or ap.shape[-1] % 2 else flat.bitcast(F32)

        def by_windows(ap):
            return ap.rearrange("c (r w k) -> c w r k", w=NW, k=WS)

        def image_rows(st, lag, dy, dx):
            at = place(st, lag)[1] * CROW + dy * PAD + dx
            return ximg[:, at:at + CROW].rearrange("c (r q) -> c r q", q=PAD)[:, :, 0:SIDE]

        block = ctx.enter_context(nc.Block())

        @block.sync
        def _(sp):
            loads = [
                (wq_f[0:C, :], w_qkv), (rows_f[96:97, :], b_qkv_row), (brow[96:97, :], b_proj_row),
                (bv_c, b_v), (wpn_f[:, :], w_proj), (g_c, ln_g), (b_c, ln_b), (bng_c, bn_g), (bnb_c, bn_b),
                (bnm_c, bn_mean), (bnv_c, bn_var), (b2_c, b2), (cw_c, conv_w), (b1_c[:, :], b1), (w1_s[:, :], w1),
                (w2_s[:, :, :], w2), (eye_f[:, :], eye),
                (bias_f[64:ROWS, 0, :], bias_q), (bias_f[64:ROWS, 1, :], bias_k), (lo_f, bias_q),
                (hot_f[64:ROWS, :], eye[0:TOK, 0:WP]),
            ]
            sp.wait_ge(pool_setup, 1)
            for w in range(2):
                for h2 in range(2):
                    loads.append((wp[48 * w:48 * w + 48, 2 * w + h2, :], w_proj2[h2]))
            for dst, src in loads:
                sp.dma_start(dst, src).then_inc(loaded, 16)
            assert len(loads) == LOADS
            sp.wait_ge(loaded, 16 * LOADS)

            def load(c):
                sp.dma_start(x_sb[:, c * CT:(c + 1) * CT], dram_rows(x, (0, 0, c * CT))).then_inc(x_in[c % 4], 16)

            load(0)
            load(1)
            for r in stored:
                sp.sem_inc(r, 16)
            sp.wait_ge(ready, 4)

            def held(v):
                return v if isinstance(v, int) else nc.sync.snap(v)

            def count(st, lag, per=1):
                u, e = st
                return held(u * (UN * per) + (e - lag + 1) * per)

            def wait_for(s, v):
                if not isinstance(v, int) or v > 0:
                    sp.wait_ge(s, v)

            def exp_parts(r2, r4, n, kk, qq):
                r0 = PIECE * (n + 1)
                sp.dma_start(k_st[r0:r0 + PIECE, r4, :, :], kk[:, r2, :]).then_inc(exp_in[r4], 16)
                for h2 in range(2):
                    sp.dma_start(q_bd[r0 + 8 * h2:r0 + 8 * h2 + 8, r4, h2::2, :],
                                 qq[48 * h2:48 * h2 + 48, r2, :]).then_inc(exp_in[r4], 16)

            def step(st):
                e = st[1]
                c1, c2, c3, c6, c8 = (count(st, lag) for lag in (1, 2, 3, 6, 8))
                x_at, out_at = dram_place(st, -2), dram_place(st, 8)
                if real(st, 2):
                    wait_for(kh_done, c2)
                    wait_for(qh_done, c2)
                    exp_parts(e % 2, (e - 2) % 4, 0, kh, qh)
                if real(st, 3):
                    wait_for(ql_done, c3)
                    exp_parts((e - 3) % 2, (e - 3) % 4, 2, kh, ql)
                    wait_for(mxt_out, c3)
                    sp.dma_start(q_bd[0:1, (e - 3) % 4, :, :].rearrange("p h (n c) -> p (h n) c", c=2 * WP),
                                 mxt[:, (e - 3) % 2, :]).then_inc(row_in[(e - 3) % 2], 16)
                if real(st, -2):
                    wait_for(sum_done, c6)
                    sp.dma_start(x_sb[:, x_at[2]:x_at[2] + CT], dram_rows(x, x_at)).then_inc(x_in[(e + 2) % 4], 16)
                if real(st, 1):
                    r2 = (e - 1) % 2
                    wait_for(kh_done, c1)
                    for w in range(2):
                        n = WP * w
                        for h2 in range(2):
                            r0 = PIECE * (1 + w) + 8 * h2
                            sp.dma_start(k_bd[r0:r0 + 8, r2, h2::2, 0:NW * WP - n], kh[48 * h2:48 * h2 + 48, r2, n:NW * WP])\
                              .then_inc(max_in[r2], 16)
                if real(st, 8):
                    wait_for(y_done, c8)
                if real(st, 1):
                    wait_for(qm_done, c1)
                    for w in range(2):
                        r0, n = PIECE * (1 + w), NW * WP * w
                        sp.dma_start(q_st[r0:r0 + PIECE, r2, :, :], qm[:, r2, n:n + NW * WP]).then_inc(max_in[r2], 16)
                if real(st, 8):
                    sp.dma_start(dram_rows(out, out_at), y[0:C, e % 2, :]).then_inc(stored[e % 2], 16)
                if real(st, 1):
                    wait_for(kl_done, c1)
                    wait_for(qh_done, c1)
                    exp_parts(r2, (e - 1) % 4, 1, kl, qh)

            run(sp, step)
            for r in stored:
                sp.wait_ge(r, 16 * (CHUNKS // 2 + 1))

        @block.tensor
        def _(pe):
            mm = nc.tensor.matmul

            def three(o, sh, sl, mh, ml, start=True, stop=True):
                mm(o, sh, mh, start=start, stop=False)
                mm(o, sh, ml, start=False, stop=False)
                return mm(o, sl, mh, start=False, stop=stop)

            pe.wait_ge(loaded, 16 * LOADS)
            mm(a_ps[96:97, 0:3 * C], b_c, wq_f[0:C, :], start=True, stop=True)
            mm(b_ps[0:C, 0:1], wq_f[0:C, 2 * C:], b_c, start=True, stop=True).then_inc(pe_setup, 1)
            pe.wait_ge(shift_done, 1)
            mm(d_ps[96:97, 0:C], bvs_c, wpn_f[:, :], start=True, stop=True).then_inc(pe_setup, 1)
            pe.wait_ge(shift_done, 2)
            for k in range(NB):
                last = mm(st_ps[:, 0, k:k + 1], w1_s[:, k * 128:(k + 1) * 128], cb_c, start=True, stop=True)
            last.then_inc(pe_setup, 1)
            pe.wait_ge(ready, 4)

            def exp_scores(st, lag, q):
                if not real(st, lag):
                    return
                r = (st[1] - lag) % 4
                if q == 0:
                    wait_ring(pe, exp_in, st, lag, 9 * 16)
                    wait_ring(pe, row_in, st, lag)
                wait(pe, ph_done, st, lag, NP, q)
                for b in range(2):
                    mm(st_ps[:, b, 0:HALF], hot2[:, :, :].rearrange("p a b -> p (a b)"), lo_l[:, b * HALF:(b + 1) * HALF],
                       start=True, stop=False, skip_group_check=True)
                for j in range(NJ):
                    for w in range(2):
                        n = (2 * q + w) * WP
                        c0 = j % (NJ // 2) * 2 * TOK
                        last = mm(st_ps[64 * w:64 * w + 64, j // (NJ // 2), c0:c0 + 2 * TOK], k_st[:, r, j, n:n + WP],
                                  q_bd[:, r, 2 * j:2 * j + 2, n:n + TOK], start=False, stop=True, skip_group_check=True)
                last.then_inc(st_done, 1)

            def max_scores(st, lag, p):
                if not real(st, lag):
                    return
                if p == 0:
                    wait_ring(pe, max_in, st, lag, 6 * 16)
                    wait(pe, mxt_out, st, lag + 1)
                wait(pe, max_done, st, lag, NP, p)
                r = (st[1] - lag) % 2
                n = 2 * p * WP
                for j in range(NJ):
                    c0 = j % (NJ // 2) * 2 * TOK
                    last = mm(sm_ps[:, j // (NJ // 2), c0:c0 + 2 * TOK], q_st[:, r, j, n:n + 2 * WP],
                              k_bd[:, r, 2 * j:2 * j + 2, n:n + TOK], start=True, stop=True)
                last.then_inc(sm_done, 1)

            def values_times_p(st, lag, q):
                if not real(st, lag):
                    return
                if q == 0:
                    wait(pe, vl_done, st, lag, 2)
                wait(pe, pl_done, st, lag, NP, q + 1)
                if q % 2 == 0:
                    wait(pe, norm_done, st, lag, 4, q)
                r, r2 = (st[1] - lag) % 4, q % 2
                for j in range(NJ):
                    o = o_ps[:, r2 * 256:r2 * 256 + 2 * HEADS * VW].rearrange("p (w h) -> p w h", w=2)[:, :, j * 2 * VW:(j + 1) * 2 * VW]

                    def moving(v):
                        return v[:, r, 2 * j:2 * j + 2, 2 * q:2 * q + 2, :].rearrange("p h w d -> p w h d")

                    s_h = ph[:, r2, 2 * j:2 * j + 2, :].rearrange("p h n -> p (h n)")
                    s_l = pl[:, r2, 2 * j:2 * j + 2, :].rearrange("p h n -> p (h n)")
                    last = three(o, s_h, s_l, moving(vh), moving(vl))
                last.then_inc(pv_done, 1)

            def centred(st):
                if not real(st, 0):
                    return
                wait_ring(pe, x_in, st, 0)
                wait(pe, ql_done, st, 1)
                r = place(st, 0)[1]
                mm(d_ps[0:C, 0:CT], center[:, :], x_sb[:, r * CT:(r + 1) * CT], start=True, stop=True).then_inc(xc_done, 1)

            def variance(st):
                if not real(st, 0):
                    return
                wait(pe, sq_done, st, 0)
                wait(pe, y_done, st, 8)
                mm(a_ps[0:C, 0:CT], avg[:, :], sq[:, :], start=True, stop=True).then_inc(var_done, 1)

            def queries(st):
                if not real(st, 1):
                    return
                wait(pe, xl_done, st, 1)
                if real(st, 8):
                    wait(pe, g_done, st, 8, NB, 2)
                r = (st[1] - 1) % 2
                three(d_ps[0:C, 0:CT], wq_h[:, 0:C], wq_l[:, 0:C], xh[:, r, :, 0:TOK], xl[:, r, :, 0:TOK]).then_inc(q_done, 1)

            def keys(st):
                if not real(st, 1):
                    return
                if real(st, 8):
                    wait(pe, g_done, st, 8, NB, 3)
                else:
                    wait(pe, kl_done, st, 2)
                    wait(pe, vl_done, st, 3, 2)
                    wait(pe, sum_done, st, 6)
                r = (st[1] - 1) % 2
                three(b_ps[0:C, 0:CT], wq_h[:, C:2 * C], wq_l[:, C:2 * C], xh[:, r, :, 0:TOK], xl[:, r, :, 0:TOK]).then_inc(k_done, 1)

            def values(st):
                if not real(st, 2):
                    return
                if real(st, 1):
                    wait(pe, kl_done, st, 1)
                else:
                    wait(pe, g_done, st, 8, NB, 3)
                r = (st[1] - 2) % 2
                for n in range(NP):
                    s_h, s_l = (t[0:C, r, 2 * n:2 * n + 2, :].rearrange("c w n -> c (w n)") for t in (xh, xl))
                    last = three(b_ps[:, 0:NP * C].rearrange("p (h n d) -> p n h d", n=NP, d=HD)[:, n], s_h, s_l, wq_h[0:C, 2 * C:], wq_l[0:C, 2 * C:])
                last.then_inc(v_done, 1)

            def channels_first(st):
                if not real(st, 4):
                    return
                wait(pe, norm_done, st, 4, 4)
                if real(st, 0):
                    wait(pe, lnv_done, st, 0)
                else:
                    wait(pe, y_done, st, 8)
                for n in range(NP):
                    last = nc.tensor.transpose(a_ps[0:C, n * 128:(n + 1) * 128], on[:, n, :], eye_f[:, :])
                last.then_inc(ot_ps_done, 1)

            def projection(st):
                if not real(st, 5):
                    return
                wait(pe, ol_done, st, 5)
                if real(st, 2):
                    wait(pe, vl_done, st, 2, 2)
                else:
                    wait(pe, g_done, st, 8, NB, 3)
                for w in range(2):
                    o = b_ps[0:C, 0:CT].rearrange("c (r n w k) -> c w n r k", r=WS, w=2, k=WS)[:, w]
                    for h2 in range(2):
                        m_h, m_l = (t[:, :, h2, 0:TOK].rearrange("c n (r k) -> c n r k", k=WS) for t in (oh, ol))
                        last = three(o, wp_h[:, 2 * w + h2, :], wp_l[:, 2 * w + h2, :], m_h, m_l,
                                     start=h2 == 0, stop=h2 == 1)
                last.then_inc(proj_done, 1)

            def hidden(st, lag, k):
                if not real(st, lag):
                    return
                if k == 0:
                    wait(pe, tap_done, st, lag, 8)
                    if real(st, 4):
                        wait(pe, ol_done, st, 4)
                    else:
                        wait(pe, y_done, st, 8)
                elif k == 1:
                    if real(st, 0):
                        wait(pe, xn_done, st, 0)
                    elif real(st, 1):
                        wait(pe, ql_done, st, 1)
                    else:
                        wait(pe, g_done, st, 8, NB, 2)
                elif real(st, 6):
                    wait(pe, sum_done, st, 6)
                t = (a_ps, d_ps, b_ps)[k]
                mm(t[:, 0:CT], w1_s[:, k * 128:(k + 1) * 128], s2[0:C, (st[1] - lag) % 2, :], start=True, stop=True)\
                    .then_inc(hid_done, 1)

            def second(st, k):
                if not real(st, 8):
                    return
                wait(pe, g_done, st, 8, NB, k + 1)
                last = mm(a_ps[0:C, 0:CT], w2_s[:, k, :], g[:, k, :], start=k == 0, stop=k == NB - 1)
                if k == NB - 1:
                    last.then_inc(mlp_done, 1)

            def maxima_rows(st):
                if not real(st, 2):
                    return
                nc.tensor.transpose(mxt_ps, mx[:, st[1] % 2, :, :].rearrange("p h n -> p (h n)"), eye_h[:, :])\
                  .then_inc(mxt_done, 1)

            def step(st):
                hidden(st, 8, 2)
                max_scores(st, 2, 0)
                exp_scores(st, 4, 3)
                queries(st)
                values_times_p(st, 4, 2)
                max_scores(st, 2, 1)
                keys(st)
                second(st, 0)
                second(st, 1)
                max_scores(st, 2, 2)
                exp_scores(st, 3, 0)
                values(st)
                second(st, 2)
                centred(st)
                exp_scores(st, 3, 1)
                values_times_p(st, 4, 3)
                variance(st)
                projection(st)
                channels_first(st)
                max_scores(st, 2, 3)
                exp_scores(st, 3, 2)
                values_times_p(st, 3, 0)
                if real(st, 2):
                    wait(pe, max_done, st, 2, NP)
                values_times_p(st, 3, 1)
                maxima_rows(st)
                hidden(st, 7, 0)
                hidden(st, 7, 1)

            run(pe, step)

        @block.scalar
        def _(act):
            af = nc.scalar.activation
            act.preload_act_table_set("natural_log_exp_and_others")
            act.wait_ge(loaded, 16 * LOADS)
            act.wait_ge(dve_setup, 1)
            af(sc_c, bnv_c, ACT.Ln, bias=eps_c).then_inc(act_setup, 1)
            act.wait_ge(act_setup, 1)
            af(sc_c, sc_c, ACT.Exp, scale=-0.5).then_inc(act_setup, 1)
            act.wait_ge(ready, 4)

            def exp_both(st, lag, q, part):
                if not real(st, lag):
                    return
                src = st_ps[:, :, 0:HALF].rearrange("p b (h n) -> p b h n", n=TOK)
                if part == 0:
                    wait(act, st_done, st, lag, NP, q + 1)
                    wait(act, pl_done, st, lag, NP, q - 1)
                    af(p32[:, q % 2, :, :].rearrange("p (b h) n -> p b h n", b=2), src, ACT.Exp)
                else:
                    wait(act, pv_done, st, lag, NP, q - 1)
                    af(ph[:, q % 2, :, 0:TOK].rearrange("p (b h) n -> p b h n", b=2), src, ACT.Exp).then_inc(ph_done, 1)

            def high_part(st, ps, dst, done, out_):
                if not real(st, 1):
                    return
                wait_ring(act, exp_in, st, 3, 9 * 16)
                wait_ring(act, max_in, st, 3, 6 * 16)
                wait(act, done, st, 1)
                af(dst[:, (st[1] - 1) % 2, :].rearrange("c (w t) -> c w t", t=WP)[:, :, 0:TOK],
                   ps[0:C, 0:CT].rearrange("c (w t) -> c w t", t=TOK), ACT.Identity, scale=1 / UP).then_inc(out_, 1)

            def masked(st):
                if not real(st, 1):
                    return
                wait(act, q_done, st, 1)
                af(qm[:, (st[1] - 1) % 2, :].rearrange("c (w n) -> c w n", w=2)[:, :, 0:NW * WP]
                   .rearrange("c w (n t) -> c n w t", n=NP)[:, :, :, 0:TOK],
                   d_ps[0:C, 0:CT].rearrange("c (n w t) -> c n w t", w=2, t=TOK), ACT.Identity, scale=1 / UP).then_inc(qm_done, 1)

            def gelu(st, lag, k):
                if not real(st, lag):
                    return
                wait(act, hid_done, st, lag, NB, k + 1)
                af(g[:, k, :], (a_ps, d_ps, b_ps)[k][:, 0:CT], ACT.Gelu, bias=b1_c[:, k:k + 1]).then_inc(g_done, 1)

            def step(st):
                gelu(st, 8, 1)
                gelu(st, 8, 2)
                if real(st, 8):
                    act.preload_act_table_set("natural_log_exp_and_others")
                exp_both(st, 4, 3, 0)
                high_part(st, b_ps, kh, k_done, kh_done)
                exp_both(st, 4, 3, 1)
                masked(st)
                high_part(st, d_ps, qh, q_done, qh_done)
                for part in range(2):
                    exp_both(st, 3, 0, part)
                if real(st, 2):
                    wait(act, v_done, st, 2)
                    wait(act, pv_done, st, 6, NP)
                    for w in range(2):
                        af(vh[64 * w:64 * w + TOK, (st[1] - 2) % 4, :, w::2, 0:HD].rearrange("p h n d -> p (h n) d"),
                           b_ps[64 * w:64 * w + TOK, 0:NP * C].rearrange("p (m d) -> p m d", d=HD),
                           ACT.Identity, scale=1 / UP).then_inc(vh_done, 1)
                if real(st, 0):
                    wait(act, xc_done, st, 0)
                    af(sq[:, :], d_ps[0:C, 0:CT], ACT.Square).then_inc(sq_done, 1)
                for part in range(2):
                    exp_both(st, 3, 1, part)
                if real(st, 0):
                    wait(act, var_done, st, 0)
                    wait(act, xn_done, st, 1)
                    af(rstd[:, :], a_ps[0:C, 0:CT], ACT.Ln, bias=eps_c).then_inc(lnv_done, 1)
                    wait(act, lnv_done, st, 0)
                    af(rstd[:, :], rstd[:, :], ACT.Exp, scale=-0.5).then_inc(rstd_done, 1)
                if real(st, 4):
                    wait(act, ot_ps_done, st, 4)
                    wait(act, proj_done, st, 5)
                    af(oh[0:C, :, :, 0:TOK], a_ps[0:C, :].rearrange("c (n a t) -> c n a t", n=NP, a=2)[:, :, :, 0:TOK],
                       ACT.Identity).then_inc(oh_done, 1)
                if real(st, 0):
                    wait(act, xn_done, st, 0)
                    wait(act, v_done, st, 2)
                    af(xh[0:C, st[1] % 2, :, 0:TOK], xn[:, :, :], ACT.Identity).then_inc(xh_done, 1)
                for part in range(2):
                    exp_both(st, 3, 2, part)
                gelu(st, 7, 0)

            run(act, step)

        @block.gpsimd
        def _(pool):
            tt = nc.gpsimd.tensor_tensor
            nc.gpsimd.memset(wp[:, :, :], 0.0).then_inc(pool_setup, 1)
            for t in (q_bd, xh, xl, oh, ol, qh, ql, kh, kl, qm, ph, pl, on, vh, vl):
                nc.gpsimd.memset(words(t[:]), 0.0)
            nc.gpsimd.memset(ximg[:, :], 0.0).then_inc(pool_setup, 1)
            pool.wait_ge(pool_setup, 2)
            nc.gpsimd.memset(xh[96:97, :, :, :], 1.0)
            nc.gpsimd.memset(oh[96:97, :, :, :], 1.0).then_inc(pool_setup, 1)
            pool.wait_ge(pool_setup, 3)
            pool.sem_inc(ready, 1)
            pool.wait_ge(ready, 4)

            def low_part(st, lag, p):
                if not real(st, lag):
                    return
                wait(pool, ph_done, st, lag, NP, p + 1)
                wait(pool, pv_done, st, lag, NP, p - 1)
                tt(pl[:, p % 2, :, 0:TOK], p32[:, p % 2, :, :], ph[:, p % 2, :, 0:TOK], ALU.subtract).then_inc(pl_done, 1)

            def step(st):
                r = (st[1] - 1) % 2
                if real(st, 1):
                    wait(pool, xh_done, st, 1)
                    tt(xl[0:C, r, :, 0:TOK], xn[:, :, :], xh[0:C, r, :, 0:TOK], ALU.subtract).then_inc(xl_done, 1)
                low_part(st, 4, 2)
                low_part(st, 4, 3)
                low_part(st, 3, 0)
                if real(st, 6):
                    wait(pool, sum_done, st, 6)
                    wait(pool, y_done, st, 8)
                    tt(s2[0:C, st[1] % 2, :].rearrange("c (r q) -> c r q", q=SIDE), image_rows(st, 6, 0, 0),
                       cw_c[:, 0:1].unsqueeze(2).broadcast_to([C, WS, SIDE]), ALU.mult).then_inc(tap0_done, 1)
                low_part(st, 3, 1)

            run(pool, step)

        @block.vector
        def _(dve):
            v = nc.vector
            at = [0]

            def link(ins):
                at[0] += 1
                ins.then_inc(dve_setup, 1)
                dve.wait_ge(dve_setup, at[0])

            link(v.memset(eps_c, EPS))
            for t in (q_st, k_st, k_bd):
                v.memset(words(t[:]), 0.0)
            v.memset(hot2[:, :, :], 0.0)
            v.memset(minus[:, :], 0.0)
            link(v.memset(avg[:, :], 1.0 / C))
            dve.wait_ge(loaded, 16 * LOADS)
            dve.wait_ge(pe_setup, 1)
            link(v.tensor_tensor(bvs_c, b_ps[0:C, 0:1], bv_c, ALU.add))
            dve.sem_inc(shift_done, 1)
            dve.wait_ge(act_setup, 2)
            link(v.tensor_tensor(sc_c, sc_c, bng_c, ALU.mult))
            link(v.tensor_tensor(cb_c, bnm_c, sc_c, ALU.mult))
            link(v.tensor_tensor(cb_c, bnb_c, cb_c, ALU.subtract))
            dve.sem_inc(shift_done, 1)
            v.tensor_scalar(cw_c, cw_c, sc_c, None, ALU.mult)
            v.tensor_tensor(b2_c, b2_c, cb_c, ALU.add)
            v.tensor_scalar(wq[0:C, :], wq_f[0:C, :], g_c, None, ALU.mult)
            v.tensor_copy(lo_h, lo_f)
            v.tensor_copy(eye_h[:, :], eye_f[:, :])
            v.tensor_scalar(center[:, :], eye_f[0:C, 0:C], -1.0 / C, None, ALU.add)
            for w in range(2):
                v.tensor_copy(hot2[:, w, 0:TOK], eye_f[0:TOK, 0:TOK])
            link(v.tensor_tensor(wq[96:97, :], a_ps[96:97, 0:3 * C], rows_f[96:97, :], ALU.add))
            link(v.tensor_scalar(wq[:, 0:C], wq[:, 0:C], SCALE, None, ALU.mult))
            v.tensor_tensor(lo_l[:, :], lo_f, lo_h, ALU.subtract)
            dve.wait_ge(pe_setup, 2)
            for w in range(2):
                v.tensor_tensor(wp[96:97, 2 * w, :], d_ps[96:97, 0:C], brow[96:97, :], ALU.add)
            dve.wait_ge(pe_setup, 3)
            link(v.tensor_tensor(b1_c[:, :], b1_c[:, :], st_ps[:, 0, 0:NB], ALU.add))
            v.tensor_scalar(wq_h[:, :], wq, UP, None, ALU.mult)
            link(v.tensor_scalar(wp_h[:, :, :], wp[:, :, :], UP, None, ALU.mult))
            v.scalar_tensor_tensor(wq_l[:, :], wq, UP, wq_h[:, :], ALU.mult, ALU.subtract)
            v.scalar_tensor_tensor(wp_l[:, :, :], wp[:, :, :], UP, wp_h[:, :, :], ALU.mult, ALU.subtract)
            v.tensor_copy(hot_h[64:ROWS, :], hot_f[64:ROWS, :])
            v.tensor_copy(bias_h[64:ROWS, :, :], bias_f[64:ROWS, :, :])
            link(v.memset(minus[:, 0:TOK], -1.0))
            for r in range(4):
                for t in (k_st, q_st)[:1 + (r < 2)]:
                    v.tensor_copy(t[64:ROWS, r, :, :].rearrange("p j (w t) -> p (j w) t", t=WP),
                                  hot_h[64:ROWS, :].unsqueeze(1).broadcast_to([TOK, NJ * NW, WP]))
                v.tensor_copy(k_st[0:1, r, :, :].rearrange("p j (w t) -> p (j w) t", t=WP),
                              minus[:, :].unsqueeze(1).broadcast_to([1, NJ * NW, WP]))
            dve.wait_ge(pool_setup, 3)
            for r in range(4):
                for t, which in ((q_bd, 0), (k_bd, 1))[:1 + (r < 2)]:
                    v.tensor_copy(t[64:ROWS, r, :, :].rearrange("p h (w t) -> p h w t", t=WP)[:, :, :, 0:TOK],
                                  bias_h[64:ROWS, which, :].rearrange("p (h t) -> p h t", t=TOK)
                                  .unsqueeze(2).broadcast_to([TOK, HEADS, NW, TOK]))
                for w in range(2):
                    last = v.memset(vh[64 * w:64 * w + TOK, r, :, w::2, HD:VW], 1.0)
            link(last)
            dve.sem_inc(ready, 3)

            def maxima(st, lag, p):
                if not real(st, lag):
                    return
                wait(dve, sm_done, st, lag, NP, p + 1)
                v.tensor_reduce(mx[:, (st[1] - lag) % 2, :, p].rearrange("p (b h) -> p b h", b=2),
                                sm_ps[:, :, 0:HALF].rearrange("p b (h n) -> p b h n", n=TOK), AX.X, ALU.max)\
                 .then_inc(max_done, 1)

            def normalise(st, lag, half):
                if not real(st, lag):
                    return
                wait(dve, pv_done, st, lag, NP, 2 * half + 2)
                wait(dve, ot_ps_done, st, lag + 1)
                o = o_ps[:, :].rearrange("p (n c) -> p n c", n=2)[:, :, 0:2 * HEADS * VW].rearrange("p n (g a d) -> p n g a d", a=2, d=VW)
                for h2 in range(2):
                    rows = slice(64 * h2, 64 * h2 + TOK)
                    v.reciprocal(rec[rows, half, :, :], o[rows, :, :, h2, HD]).then_inc(rec_done, 1)
                for h2 in range(2):
                    rows = slice(64 * h2, 64 * h2 + TOK)
                    wait(dve, rec_done, st, lag, 4, 2 * half + h2 + 1)
                    v.tensor_tensor(on[rows, 2 * half:2 * half + 2, :].rearrange("p n (g d) -> p n g d", d=HD),
                                    o[rows, :, :, h2, 0:HD], rec[rows, half, :, :].unsqueeze(3).broadcast_to([TOK, 2, HEADS, HD]),
                                    ALU.mult).then_inc(norm_done, 1)

            def tap(st, lag, k):
                if not real(st, lag):
                    return
                acc = s2[0:C, (st[1] - lag) % 2, :].rearrange("c (r q) -> c r q", q=SIDE)
                if k == 1:
                    wait(dve, tap0_done, st, lag)
                else:
                    wait(dve, tap_done, st, lag, 8, k - 1)
                if k == 6 and real(st, 6):
                    wait(dve, sum_done, st, 6)
                v.scalar_tensor_tensor(acc, image_rows(st, lag, k // 3, k % 3), cw_c[:, k:k + 1], acc, ALU.mult, ALU.add)\
                 .then_inc(tap_done, 1)

            def low_part(st, ps, hi, dst, done, out_):
                if not real(st, 1):
                    return
                wait(dve, done, st, 1)
                r = (st[1] - 1) % 2
                v.scalar_tensor_tensor(dst[:, r, :].rearrange("c (w t) -> c w t", t=WP)[:, :, 0:TOK],
                                       ps[0:C, 0:CT].rearrange("c (w t) -> c w t", t=TOK), 1 / UP,
                                       hi[:, r, :].rearrange("c (w t) -> c w t", t=WP)[:, :, 0:TOK],
                                       ALU.mult, ALU.subtract).then_inc(out_, 1)

            def step(st):
                e = st[1]
                tap(st, 7, 2)
                maxima(st, 2, 0)
                tap(st, 7, 3)
                tap(st, 7, 4)
                maxima(st, 2, 1)
                tap(st, 7, 5)
                low_part(st, b_ps, kh, kl, kh_done, kl_done)
                tap(st, 7, 6)
                low_part(st, d_ps, qh, ql, qh_done, ql_done)
                maxima(st, 2, 2)
                tap(st, 7, 7)
                if real(st, 8):
                    wait(dve, mlp_done, st, 8)
                    wait_ring(dve, stored, st, 8)
                    v.scalar_tensor_tensor(y[0:C, e % 2, :], a_ps[0:C, 0:CT], b2_c, s2[0:C, e % 2, :], ALU.add, ALU.add)\
                     .then_inc(y_done, 1)
                if real(st, 2):
                    for w in range(2):
                        wait(dve, vh_done, st, 2, 2, w + 1)
                        hi, lo = (t[64 * w:64 * w + TOK, (e - 2) % 4, :, w::2, 0:HD].rearrange("p h n d -> p (h n) d") for t in (vh, vl))
                        v.scalar_tensor_tensor(lo, b_ps[64 * w:64 * w + TOK, 0:NP * C].rearrange("p (m d) -> p m d", d=HD), 1 / UP, hi,
                                               ALU.mult, ALU.subtract).then_inc(vl_done, 1)
                normalise(st, 4, 1)
                tap(st, 7, 8)
                if real(st, 0):
                    wait(dve, rstd_done, st, 0)
                    wait(dve, xl_done, st, 1)
                    v.tensor_tensor(xn[:, :, :].rearrange("c w (r k) -> c w r k", k=WS), by_windows(d_ps[0:C, 0:CT]),
                                    by_windows(rstd[:, :]), ALU.mult).then_inc(xn_done, 1)
                maxima(st, 2, 3)
                if real(st, 4):
                    wait(dve, oh_done, st, 4)
                    v.tensor_tensor(ol[0:C, :, :, 0:TOK], a_ps[0:C, :].rearrange("c (n a t) -> c n a t", n=NP, a=2)[:, :, :, 0:TOK],
                                    oh[0:C, :, :, 0:TOK], ALU.subtract).then_inc(ol_done, 1)
                tap(st, 6, 1)
                if real(st, 5):
                    wait(dve, proj_done, st, 5)
                    r = place(st, 5)[1]
                    at = r * CROW + PAD + 1
                    v.scalar_tensor_tensor(ximg[:, at:at + CROW].rearrange("c (r q) -> c r q", q=PAD)[:, :, 0:SIDE],
                                           b_ps[0:C, 0:CT].rearrange("c (r q) -> c r q", q=SIDE), 1 / UP,
                                           x_sb[:, r * CT:(r + 1) * CT].rearrange("c (r q) -> c r q", q=SIDE),
                                           ALU.mult, ALU.add).then_inc(sum_done, 1)
                if real(st, 2):
                    wait(dve, mxt_done, st, 2)
                    wait_ring(dve, row_in, st, 4)
                    v.tensor_copy(mxt[:, e % 2, :], mxt_ps).then_inc(mxt_out, 1)
                normalise(st, 3, 0)

            run(dve, step)


def kernel(x, L0_conv_ln_g, L0_conv_ln_b, L0_conv_qkv_w, L0_conv_qkv_b, L0_conv_proj_w, L0_conv_proj_b,
           L0_conv_bias_table, L0_conv_conv_w, L0_conv_bn_g, L0_conv_bn_b, L0_conv_bn_mean, L0_conv_bn_var,
           L0_conv_w1, L0_conv_b1, L0_conv_w2, L0_conv_b2):
    import concourse.bacc as bacc
    from concourse.bass_utils import run_bass_kernel_spmd

    def a(v):
        return np.asarray(v)

    order = np.arange(C).reshape(NJ, 2, HD).transpose(1, 2, 0).reshape(-1)
    perm = np.concatenate([order, C + order, 2 * C + np.arange(C)])
    at = np.stack(np.meshgrid(np.arange(WS), np.arange(WS), indexing="ij"), -1).reshape(-1, 2)
    rel = at[:, None] - at[None] + WS - 1
    bias = a(L0_conv_bias_table)[rel[..., 0] * (2 * WS - 1) + rel[..., 1]]
    w_qkv, b_qkv, w_proj = a(L0_conv_qkv_w), a(L0_conv_qkv_b), a(L0_conv_proj_w).T
    col = lambda v: a(v).reshape(C, 1)
    arrays = {
        "x": a(x),
        "w_qkv": w_qkv.T[:, perm],
        "b_qkv_row": b_qkv[perm].reshape(1, -1),
        "b_v": col(b_qkv[2 * C:]),
        "w_proj": w_proj,
        "w_proj2": w_proj.reshape(NJ, 2, HD, C).transpose(1, 0, 2, 3).reshape(2, C // 2, C),
        "b_proj_row": a(L0_conv_proj_b).reshape(1, C),
        "ln_g": col(L0_conv_ln_g), "ln_b": col(L0_conv_ln_b),
        "bias_q": bias.transpose(1, 2, 0).reshape(TOK, -1),
        "bias_k": bias.transpose(0, 2, 1).reshape(TOK, -1),
        "conv_w": a(L0_conv_conv_w).reshape(C, 9),
        "bn_g": col(L0_conv_bn_g), "bn_b": col(L0_conv_bn_b), "bn_mean": col(L0_conv_bn_mean), "bn_var": col(L0_conv_bn_var),
        "w1": a(L0_conv_w1).T, "b1": a(L0_conv_b1).reshape(NB, 128).T,
        "w2": a(L0_conv_w2).T.reshape(NB, 128, C).transpose(1, 0, 2), "b2": col(L0_conv_b2),
        "eye": np.eye(128, dtype=np.float32),
    }
    arrays = {f"in_{k}": np.ascontiguousarray(v) for k, v in arrays.items()}
    nc = bacc.Bacc("TRN2", target_bir_lowering=False, num_devices=1)
    args = [nc.dram_tensor(k, v.shape, mybir.dt.from_np(v.dtype), kind="ExternalInput").ap() for k, v in arrays.items()]
    args.append(nc.dram_tensor("out_0", (BATCH, C, SIDE, SIDE), F32, kind="ExternalOutput").ap())
    block_program(nc, *args)
    r = run_bass_kernel_spmd(nc, [arrays], core_ids=[0])
    return r.results[0]["out_0"]
```
